# Optimizing a Trainium2 kernel written in Bass

```python
import numpy as np
import jax
import jax.numpy as jnp

def _softmax(x, axis=-1):
    return jax.nn.softmax(x, axis=axis)

def _gelu(x):
    return jax.nn.gelu(x, approximate=True)

def _silu(x):
    return jax.nn.silu(x)

def _sigmoid(x):
    return jax.nn.sigmoid(x)

def _layernorm(x, axis=-1, eps=1e-05):
    m = jnp.mean(x, axis=axis, keepdims=True)
    v = jnp.var(x, axis=axis, keepdims=True)
    return (x - m) / jnp.sqrt(v + eps)

def _scatter_add(tgt, idx, src, axis=0):
    return tgt.at[idx].add(src)

def _segment_sum(src, seg, n):
    return jax.ops.segment_sum(src, seg, n)
kernel_name = 'mk_adaln_ffn_d2_seqx_r8_348193'

def setup_inputs(seed: int=0):
    np.random.seed(seed)
    _w = jnp.asarray

    def _rec_inputs():
        import jax
        import jax.numpy as jnp
        _rk = jax.random.key(seed)
        x = 0.0001734 + 0.8201 * jax.random.normal(jax.random.fold_in(_rk, 1), (64, 32, 512), jnp.float32)
        _lenS = 32 - jax.random.randint(jax.random.fold_in(_rk, 7), (64,), 0, max(1, 32 // 4) + 1, jnp.int32)
        _lenS2 = 32 - jax.random.randint(jax.random.fold_in(_rk, 8), (64,), 0, max(1, 32 // 4) + 1, jnp.int32)
        itok_B_0_7 = jax.random.randint(jax.random.fold_in(_rk, 11), (64,), 0, 8, jnp.int32)
        itok_B_2182_4065 = jax.random.randint(jax.random.fold_in(_rk, 13), (64,), 2182, 4066, jnp.int32)
        return (x, itok_B_0_7, itok_B_2182_4065, _lenS)
    x, itok_B_0_7, itok_B_2182_4065, _lenS = _rec_inputs()

    def _L0_cond_setup():
        import jax, jax.numpy as jnp
        import numpy as np
        SESSION_CHANNELS = [128, 160, 192, 224, 240, 248, 252, 32]
        N_SESS = len(SESSION_CHANNELS)
        B, MAX_C, MAX_T = (16, 32, 512)
        HID, N_SRC = (64, 32)
        key = jax.random.key(seed)
        ks = jax.random.split(key, 7)
        session_ids = jax.random.randint(ks[0], (B,), 0, N_SESS)
        chan_table = jnp.asarray(SESSION_CHANNELS)
        channel_counts = chan_table[session_ids]
        seq_lens = jax.random.randint(ks[1], (B,), MAX_T // 2, MAX_T + 1)
        x = jax.random.normal(ks[2], (B, MAX_C, MAX_T), jnp.float32)
        cmask = (jnp.arange(MAX_C)[None, :] < channel_counts[:, None]).astype(x.dtype)
        tmask = (jnp.arange(MAX_T)[None, :] < seq_lens[:, None]).astype(x.dtype)
        x = x * cmask[:, :, None] * tmask[:, None, :]
        lim1 = 1.0 / np.sqrt(MAX_C)
        W_sess = jax.random.uniform(ks[3], (N_SESS, MAX_C, HID), jnp.float32, -lim1, lim1)
        b_sess = jax.random.uniform(ks[4], (N_SESS, HID), jnp.float32, -lim1, lim1)
        lim2 = 1.0 / np.sqrt(HID)
        W2 = jax.random.uniform(ks[5], (HID, N_SRC), jnp.float32, -lim2, lim2)
        b2 = jax.random.uniform(ks[6], (N_SRC,), jnp.float32, -lim2, lim2)
        return dict(x=x, session_ids=session_ids, channel_counts=channel_counts, seq_lens=seq_lens, W_sess=W_sess, b_sess=b_sess, W2=W2, b2=b2)
    _L0_cond_all = _L0_cond_setup()
    _L0_cond_in = {k: v for k, v in _L0_cond_all.items() if k in ('W_sess', 'b_sess', 'W2', 'b2')}
    del _L0_cond_all

    def _L0_ffn_setup():
        import jax, jax.numpy as jnp
        import numpy as np
        LORA_R = 16
        SCALE = 16.0 / np.sqrt(16.0)
        NUM_EXPERTS = 4
        TOP_K = 2
        IN_F = 512
        OUT_F = 512
        key = jax.random.key(seed)
        k_x, k_a, k_b, k_r = jax.random.split(key, 4)
        x = jax.random.normal(k_x, (2, 256, IN_F), dtype=jnp.float32)
        A = jax.random.normal(k_a, (NUM_EXPERTS, LORA_R, IN_F), dtype=jnp.float32) * (1.0 / np.sqrt(IN_F))
        B = jax.random.normal(k_b, (NUM_EXPERTS, OUT_F, LORA_R), dtype=jnp.float32) * 0.02
        Wr = jax.random.normal(k_r, (NUM_EXPERTS, IN_F), dtype=jnp.float32) * 0.02
        return {'x': x, 'A': A, 'B': B, 'Wr': Wr}
    _L0_ffn_all = _L0_ffn_setup()
    _L0_ffn_in = {k: v for k, v in _L0_ffn_all.items() if k in ('A', 'B', 'Wr')}
    del _L0_ffn_all

    def _L1_cond_setup():
        import jax, jax.numpy as jnp
        import numpy as np
        TOP_K = 2
        LANG_BIAS = 5.0
        SCALING = 32.0 / 16.0
        LANGUAGE_PAD_ID = -1
        key = jax.random.key(seed)
        ks = jax.random.split(key, 6)
        B, T, D, O, E, R = (4, 256, 512, 512, 8, 16)
        x = jax.random.normal(ks[0], (B, T, D), dtype=jnp.float32)
        language_ids = jax.random.randint(ks[1], (B,), 0, E).astype(jnp.int64)
        W = jax.random.normal(ks[2], (O, D), dtype=jnp.float32) * (1.0 / np.sqrt(D))
        Wr = jax.random.normal(ks[3], (E, D), dtype=jnp.float32) * (1.0 / np.sqrt(D))
        A = jax.random.normal(ks[4], (E, R, D), dtype=jnp.float32) * (1.0 / np.sqrt(D))
        Bm = jax.random.normal(ks[5], (O, R), dtype=jnp.float32) * 0.0
        Bm = jnp.broadcast_to(Bm, (E, O, R)) + jax.random.normal(ks[5], (E, O, R), dtype=jnp.float32) * 0.02
        return {'x': x, 'language_ids': language_ids, 'W': W, 'Wr': Wr, 'A': A, 'B': Bm}
    _L1_cond_all = _L1_cond_setup()
    _L1_cond_in = {k: v for k, v in _L1_cond_all.items() if k in ('W', 'Wr', 'A', 'B')}
    del _L1_cond_all

    def _L1_ffn_setup():
        import math
        import jax, jax.numpy as jnp
        import numpy as np
        SCALING = 16.0 / 32.0

        def real_fourier_orthogonal_multiply(c):
            n = c.shape[-1]
            sqrt_n = math.sqrt(n)
            pair_scale = math.sqrt(n / 2.0)
            max_f = (n - 1) // 2
            work = c.astype(jnp.float32)
            dc = (work[..., 0] * sqrt_n)[..., None].astype(jnp.complex64)
            cos = work[..., 1:1 + 2 * max_f:2] * pair_scale
            sin = work[..., 2:2 + 2 * max_f:2] * pair_scale
            mid = (cos - 1j * sin).astype(jnp.complex64)
            parts = [dc, mid]
            if n % 2 == 0:
                parts.append((work[..., -1] * sqrt_n)[..., None].astype(jnp.complex64))
            spectrum = jnp.concatenate(parts, axis=-1)
            return jnp.fft.irfft(spectrum, n=n, axis=-1).astype(c.dtype)
        key = jax.random.key(seed)
        ks = jax.random.split(key, 9)
        B, S, D_in, D_out, R0, R1, E = (4, 256, 512, 512, 32, 8, 3)
        x = jax.random.normal(ks[0], (B, S, D_in), dtype=jnp.float32)
        W_base = jax.random.normal(ks[1], (D_out, D_in), dtype=jnp.float32) * 0.02
        b_base = jax.random.normal(ks[2], (D_out,), dtype=jnp.float32) * 0.02
        enc0 = jax.random.normal(ks[3], (R0, D_in), dtype=jnp.float32) * 0.02
        enc1 = jax.random.normal(ks[4], (R1, D_in), dtype=jnp.float32) * 0.02
        coefs0 = jax.random.normal(ks[5], (E, D_out, R0), dtype=jnp.float32) * 0.02
        coefs1 = jax.random.normal(ks[6], (E, D_out, R1), dtype=jnp.float32) * 0.02
        mask0 = jax.random.randint(ks[7], (E, D_out, R0), 0, 2).astype(bool)
        mask1 = jax.random.randint(ks[8], (E, D_out, R1), 0, 2).astype(bool)
        return dict(x=x, W_base=W_base, b_base=b_base, enc0=enc0, enc1=enc1, coefs0=coefs0, coefs1=coefs1, mask0=mask0, mask1=mask1)
    _L1_ffn_all = _L1_ffn_setup()
    _L1_ffn_in = {k: v for k, v in _L1_ffn_all.items() if k in ('W_base', 'b_base', 'enc0', 'enc1', 'coefs0', 'coefs1', 'mask0', 'mask1')}
    del _L1_ffn_all
    return {'x': x, 'itok_B_0_7': itok_B_0_7, 'itok_B_2182_4065': itok_B_2182_4065, '_lenS': _lenS, 'L0_cond_W_sess': _L0_cond_in['W_sess'], 'L0_cond_b_sess': _L0_cond_in['b_sess'], 'L0_cond_W2': _L0_cond_in['W2'], 'L0_cond_b2': _L0_cond_in['b2'], 'L0_ffn_A': _L0_ffn_in['A'], 'L0_ffn_B': _L0_ffn_in['B'], 'L0_ffn_Wr': _L0_ffn_in['Wr'], 'L1_cond_W': _L1_cond_in['W'], 'L1_cond_Wr': _L1_cond_in['Wr'], 'L1_cond_A': _L1_cond_in['A'], 'L1_cond_B': _L1_cond_in['B'], 'L1_ffn_W_base': _L1_ffn_in['W_base'], 'L1_ffn_b_base': _L1_ffn_in['b_base'], 'L1_ffn_enc0': _L1_ffn_in['enc0'], 'L1_ffn_enc1': _L1_ffn_in['enc1'], 'L1_ffn_coefs0': _L1_ffn_in['coefs0'], 'L1_ffn_coefs1': _L1_ffn_in['coefs1'], 'L1_ffn_mask0': _L1_ffn_in['mask0'], 'L1_ffn_mask1': _L1_ffn_in['mask1']}

def reference(x, itok_B_0_7, itok_B_2182_4065, _lenS, L0_cond_W_sess, L0_cond_b_sess, L0_cond_W2, L0_cond_b2, L0_ffn_A, L0_ffn_B, L0_ffn_Wr, L1_cond_W, L1_cond_Wr, L1_cond_A, L1_cond_B, L1_ffn_W_base, L1_ffn_b_base, L1_ffn_enc0, L1_ffn_enc1, L1_ffn_coefs0, L1_ffn_coefs1, L1_ffn_mask0, L1_ffn_mask1):
    import jax
    import jax.numpy as jnp

    def _L0_cond_ref(x, session_ids, channel_counts, seq_lens, W_sess, b_sess, W2, b2):
        import jax, jax.numpy as jnp
        import numpy as np
        SESSION_CHANNELS = [128, 160, 192, 224, 240, 248, 252, 32]
        N_SESS = len(SESSION_CHANNELS)
        B, MAX_C, MAX_T = (16, 32, 512)
        HID, N_SRC = (64, 32)
        cmask = (jnp.arange(x.shape[1])[None, :] < channel_counts[:, None]).astype(x.dtype)
        xm = x * cmask[:, :, None]
        W = W_sess[session_ids]
        b = b_sess[session_ids]
        h = jnp.einsum('bct,bch->bht', xm, W) + b[:, :, None]
        h = jax.nn.gelu(h, approximate=False)
        out = jnp.einsum('bht,hs->bst', h, W2) + b2[None, :, None]
        tmask = (jnp.arange(x.shape[2])[None, :] < seq_lens[:, None]).astype(x.dtype)
        return out * tmask[:, None, :]

    def _L0_ffn_ref(x, A, B, Wr):
        import jax, jax.numpy as jnp
        import numpy as np
        LORA_R = 16
        SCALE = 16.0 / np.sqrt(16.0)
        NUM_EXPERTS = 4
        TOP_K = 2
        IN_F = 512
        OUT_F = 512
        orig_shape = x.shape
        flat = x.reshape(-1, orig_shape[-1])
        logits = flat @ Wr.T
        topk_vals, topk_idx = jax.lax.top_k(logits, TOP_K)
        T = flat.shape[0]
        neg_inf = jnp.finfo(logits.dtype).min
        sparse = jnp.full_like(logits, neg_inf)
        rows = jnp.arange(T)[:, None]
        sparse = sparse.at[rows, topk_idx].set(topk_vals)
        gates = jax.nn.softmax(sparse, axis=-1)
        mid = jnp.einsum('tf,erf->ter', flat, A)
        all_deltas = jnp.einsum('ter,eor->teo', mid, B) * SCALE
        delta = jnp.sum(gates[:, :, None] * all_deltas, axis=1)
        return delta.reshape(*orig_shape[:-1], -1)

    def _L1_cond_ref(x, language_ids, W, Wr, A, B):
        import jax, jax.numpy as jnp
        import numpy as np
        TOP_K = 2
        LANG_BIAS = 5.0
        SCALING = 32.0 / 16.0
        LANGUAGE_PAD_ID = -1
        base = jnp.einsum('btd,od->bto', x, W)
        E = Wr.shape[0]
        logits = jnp.einsum('btd,ed->bte', x.astype(jnp.float32), Wr.astype(jnp.float32))
        expert_targets = language_ids
        valid = expert_targets >= 0
        tgt = jnp.where(valid, expert_targets, 0)
        bias = jax.nn.one_hot(tgt, E, dtype=logits.dtype) * LANG_BIAS
        bias = jnp.where(valid[:, None], bias, 0.0)
        logits = logits + bias[:, None, :]
        topw, topi = jax.lax.top_k(logits, TOP_K)
        weights = jax.nn.softmax(topw, axis=-1)
        gates = jnp.sum(jax.nn.one_hot(topi, E, dtype=weights.dtype) * weights[..., None], axis=-2)
        gates = gates.astype(x.dtype)
        h = jnp.einsum('btd,erd->bter', x, A)
        lora_out = jnp.einsum('bter,bte,eor->bto', h, gates, B)
        return base + SCALING * lora_out

    def _L1_ffn_ref(x, W_base, b_base, enc0, enc1, coefs0, coefs1, mask0, mask1):
        import math
        import jax, jax.numpy as jnp
        import numpy as np
        SCALING = 16.0 / 32.0

        def real_fourier_orthogonal_multiply(c):
            n = c.shape[-1]
            sqrt_n = math.sqrt(n)
            pair_scale = math.sqrt(n / 2.0)
            max_f = (n - 1) // 2
            work = c.astype(jnp.float32)
            dc = (work[..., 0] * sqrt_n)[..., None].astype(jnp.complex64)
            cos = work[..., 1:1 + 2 * max_f:2] * pair_scale
            sin = work[..., 2:2 + 2 * max_f:2] * pair_scale
            mid = (cos - 1j * sin).astype(jnp.complex64)
            parts = [dc, mid]
            if n % 2 == 0:
                parts.append((work[..., -1] * sqrt_n)[..., None].astype(jnp.complex64))
            spectrum = jnp.concatenate(parts, axis=-1)
            return jnp.fft.irfft(spectrum, n=n, axis=-1).astype(c.dtype)
        base = jnp.einsum('bsd,od->bso', x, W_base) + b_base
        e0 = jnp.einsum('bsd,rd->bsr', x, enc0)
        e1 = jnp.einsum('bsd,rd->bsr', x, enc1)
        w0 = coefs0 * mask0.astype(coefs0.dtype)
        w1 = coefs1 * mask1.astype(coefs1.dtype)
        decoded = jnp.einsum('bsr,eor->ebso', e0, w0) + jnp.einsum('bsr,eor->ebso', e1, w1)
        transformed = real_fourier_orthogonal_multiply(decoded)
        update = transformed.sum(axis=0)
        return base + update * SCALING
    x = x + _L0_ffn_ref(_L0_cond_ref(x, itok_B_0_7, _lenS, itok_B_2182_4065, L0_cond_W_sess, L0_cond_b_sess, L0_cond_W2, L0_cond_b2), L0_ffn_A, L0_ffn_B, L0_ffn_Wr)
    x = x + _L1_ffn_ref(_L1_cond_ref(x, itok_B_0_7, L1_cond_W, L1_cond_Wr, L1_cond_A, L1_cond_B), L1_ffn_W_base, L1_ffn_b_base, L1_ffn_enc0, L1_ffn_enc1, L1_ffn_coefs0, L1_ffn_coefs1, L1_ffn_mask0, L1_ffn_mask1)
    return x

_drawn_inputs = setup_inputs


def setup_inputs(seed=0):
    import zlib

    import numpy as np

    out = dict(_drawn_inputs(seed))
    spreads = {}
    factors = {'L0_cond_b_sess': 3.636, 'L1_cond_Wr': 8.0, 'L1_ffn_enc1': 3.871, 'L1_ffn_coefs1': 4.098}
    for name, (base, spread) in spreads.items():
        noise = np.random.default_rng([zlib.crc32(name.encode()), seed]).standard_normal(out[name].shape)
        drawn = base * np.exp(spread * noise) if base else spread * noise
        out[name] = jnp.asarray(drawn.astype(out[name].dtype))
    for name, factor in factors.items():
        out[name] = (out[name] * factor).astype(out[name].dtype)
    return out
```

```python
from contextlib import ExitStack

import numpy as np

import concourse.bass as bass
from concourse import mybir


class Tile:

    def __init__(self, n, c, ring, total):
        self.n, self.c, self.ring, self.total = n, c, ring, total
        self.slot = c % ring

    def __add__(self, d):
        return Tile(self.n, self.c + d, self.ring, self.total)

    def __sub__(self, d):
        return self + (-d)

    @property
    def real(self):
        return self.n is not None or 0 <= self.c < self.total

    def count(self, per_tile=1, more=0):
        if self.n is None:
            return per_tile * self.c + more
        return self.n * (per_tile * self.ring) + (per_tile * self.c + more)

    def round(self, per_round, more=0):
        if self.n is None:
            return per_round * (self.c // self.ring) + more
        return self.n * per_round + (per_round * (self.c // self.ring) + more)

    def after(self, d):
        return self.n is not None or self.c >= d


def run_tiles(eng, ring, total, first, last, body):
    head = 2 * ring - 1
    rounds = (total - 2 - head) // ring
    stop = head + rounds * ring
    for c in range(first, head):
        body(Tile(None, c, ring, total))
    with eng.Fori(0, rounds) as n:
        for c in range(head, head + ring):
            body(Tile(n, c, ring, total))
    for c in range(stop, last + 1):
        body(Tile(None, c, ring, total))


def adaln_ffn(nc, x, session_ids, seq_lens, channel_counts, W_sess, b_sess, W2, b2, A0, B0, Wr0,
              W, Wr1, A1, B1, W_base, b_base, enc0, enc1, coefs0, coefs1, mask0, mask1, dft, out):
    fp32, f32r = mybir.dt.float32, mybir.dt.float32r
    i32, u8 = mybir.dt.int32, mybir.dt.uint8
    ALU = mybir.AluOpType
    ACT = mybir.ActivationFunctionType
    X = mybir.AxisListType.X
    ds = bass.ds

    NB, C, T = x.shape
    S, _, H = W_sess.shape
    P = 128
    QB = P // C
    NT = NB // QB
    NC = T // P
    E0, R = A0.shape[0], A0.shape[1]
    E1 = A1.shape[0]
    D = T
    K0, K1 = E0 * R, E1 * R
    NM = K0 + E0
    R0, R1 = enc0.shape[0], enc1.shape[0]
    RE = R0 + R1
    NE = coefs0.shape[0]
    L1C = K1 + E1
    NX = L1C + D
    HX = NX // 2
    OA = HX - L1C
    LANG_BIAS, SCALE0, SCALE1, NEG = 5.0, 4.0, 2.0, -3.0e38

    x_tiles = x.rearrange("(g b) c t -> (b c) g t", b=QB)
    out_tiles = out.rearrange("(g b) c t -> (b c) g t", b=QB)

    ctx = ExitStack()
    with ctx:
        def sb(name, shape, dt=fp32):
            return ctx.enter_context(nc.sbuf_tensor(name, shape, dt))

        def sem(name):
            return ctx.enter_context(nc.semaphore(name))

        bank = [ctx.enter_context(nc.psum_tensor(f"bank{k}", [P, 512], fp32)) for k in range(8)]

        ident = sb("ident", [P, P])
        delta = sb("delta", [P, C])
        quad = sb("quad", [P, QB])
        p_col = sb("p_col", [P, 1])
        t_col = sb("t_col", [P, NC])
        quad_no = sb("quad_no", [P, 1])
        quad_tmp = sb("quad_tmp", [P, 2])
        in_quad = sb("in_quad", [P, 1])
        rev0 = sb("rev0", [P, E0])
        rev1 = sb("rev1", [P, E1])
        lane1 = sb("lane1", [P, E1])

        id_b = sb("id_b", [P, NB], i32)
        cc_b = sb("cc_b", [P, NB], i32)
        sl_b = sb("sl_b", [P, NB], i32)
        id_tok = sb("id_tok", [P, NT])
        t_mask = sb("t_mask", [P, NC, NB])
        id_eq = sb("id_eq", [P, 2, NB])
        id_sel = sb("id_sel", [P, 2, NB])
        select = sb("select", [P, 2 * NB, C])
        one_hot = sb("one_hot", [S, NB])

        w_sess = sb("w_sess", [P, 2, H])
        b_sess2 = sb("b_sess2", [S, 2, H])
        w_sel = sb("w_sel", [P, NT, H])
        w_selh = sb("w_selh", [P, NT, H], f32r)
        w_sell = sb("w_sell", [P, NT, H])
        h_bias = sb("h_bias", [P, NB // 2])
        w2_blk = sb("w2_blk", [P, 2 * C])
        b2_b = sb("b2_b", [P, C])
        routers = sb("routers", [NM + E1, D])
        routersT = sb("routersT", [P, NC, NM + E1])

        w_nat = sb("w_nat", [P, NC, D])
        wbase_nat = sb("wbase_nat", [P, NC, D])
        dft_sb = sb("dft_sb", [P, NC, D])
        enc = sb("enc", [P, D])
        coef = sb("coef", [P, NE, NC, RE])
        mask = sb("mask", [P, NE, NC, RE], u8)
        wsum = sb("wsum", [P, NC, P])
        g_t = sb("g_t", [P, D])
        wb_t = sb("wb_t", [P, NC, D])
        a1_nat = sb("a1_nat", [P, D])
        b1_t = sb("b1_t", [P, NC, K1])
        b0_t = sb("b0_t", [P, NC, K0])
        b0_dup = sb("b0_dup", [P, NC, 2, K0])
        b1_scaled = sb("b1_scaled", [P, NC, K1])
        mx = sb("mx", [P, NC, NX])
        mxh = sb("mxh", [P, NC, NX], f32r)
        mxl = sb("mxl", [P, NC, NX], f32r)
        bmh = sb("bmh", [P, NX], f32r)
        bml = sb("bml", [P, NX], f32r)
        m2h = sb("m2h", [P, D], f32r)
        m2l = sb("m2l", [P, D], f32r)
        bias_b = sb("bias_b", [P, D])

        xn = sb("xn", [P, 2, T])
        xh = [sb(f"xh{k}", [P, T], f32r) for k in range(2)]
        xl = [sb(f"xl{k}", [P, T], f32r) for k in range(2)]
        wbh = [sb(f"wbh{k}", [P, QB, H], f32r) for k in range(2)]
        wbl = [sb(f"wbl{k}", [P, QB, H], f32r) for k in range(2)]
        hact = sb("hact", [P, 2, 2, T])
        ysum = sb("ysum", [P, 2, NC, QB, C])
        y0 = sb("y0", [P, 2, NC, QB, C])
        mid = sb("mid", [P, NT, NM])

        r0 = [sb(f"r0_{k}", [P, NT, E0]) for k in range(7)]
        s0 = [sb(f"s0_{k}", [P, NT]) for k in range(8)]
        gates0 = sb("gates0", [P, NT, E0])
        lang = sb("lang", [P, NT, E1])

        xs = sb("xs", [P, 3, T])
        xth = [sb(f"xth{k}", [P, NC, P], f32r) for k in range(3)]
        xtl = [sb(f"xtl{k}", [P, NC, P], f32r) for k in range(3)]
        gm = sb("gm", [P, 3, 2, K0])
        gmt = [sb(f"gmt{k}", [P, P], f32r) for k in range(3)]
        gh = sb("gh", [P, 3, K1])
        ght_h = [sb(f"ght_h{k}", [P, P], f32r) for k in range(3)]
        ght_l = [sb(f"ght_l{k}", [P, P], f32r) for k in range(3)]
        r1 = [sb(f"r1_{k}", [P, E1]) for k in range(8)]
        s1 = [sb(f"s1_{k}", [P, 1]) for k in range(9)]
        o_sb = sb("o_sb", [P, 3, D])

        lens_in, sess_in, bsess_in, w2_in, b2_in = map(sem, ("lens_in", "sess_in", "bsess_in", "w2_in", "b2_in"))
        routers_in, coef_in, dft_in, enc_in = map(sem, ("routers_in", "coef_in", "dft_in", "enc_in"))
        wbase_in, w_in, a1_in, b1_in, b0_in, bias_in = map(sem, ("wbase_in", "w_in", "a1_in", "b1_in", "b0_in", "bias_in"))
        zeroed, consts, ident_ready = sem("zeroed"), sem("consts"), sem("ident_ready")
        prep, select_ready, bias_hot = sem("prep"), sem("select_ready"), sem("bias_hot")
        wsel_done, hbias_done, routers_done = sem("wsel_done"), sem("hbias_done"), sem("routers_done")
        wsel_saved, wsel_split, hbias_saved = sem("wsel_saved"), sem("wsel_split"), sem("hbias_saved")
        routersT_saved, wsum_ready, b_scaled = sem("routersT_saved"), sem("wsum_ready"), sem("b_scaled")
        wsum_step = sem("wsum_step")
        x1_in = [sem(f"x1_in{k}") for k in range(2)]
        xh_ready, xl_ready, wb_ready = sem("xh_ready"), sem("xl_ready"), sem("wb_ready")
        a_done, h_ready = sem("a_done"), sem("h_ready")
        y_done, ysum_ready, y0_ready = sem("y_done"), sem("ysum_ready"), sem("y0_ready")
        mid_done, mid_saved = sem("mid_done"), sem("mid_saved")
        g_done, g_saved, wb_done, wb_saved = sem("g_done"), sem("g_saved"), sem("wb_done"), sem("wb_saved")
        a1t_done, a1t_saved, m1_done, m1_saved = sem("a1t_done"), sem("a1t_saved"), sem("m1_done"), sem("m1_saved")
        mx_ready, mxh_ready, mxl_ready, wr1_saved = sem("mx_ready"), sem("mxh_ready"), sem("mxl_ready"), sem("wr1_saved")
        m2_done, m2h_ready, m2l_ready = sem("m2_done"), sem("m2h_ready"), sem("m2l_ready")
        bm_done, bmh_ready, bml_ready = sem("bm_done"), sem("bmh_ready"), sem("bml_ready")
        route0, gap0_ready, exp0_ready, gates0_ready = sem("route0"), sem("gap0_ready"), sem("exp0_ready"), sem("gates0_ready")
        x2_in = [sem(f"x2_in{k}") for k in range(3)]
        xt_done, xth_ready, xtl_ready = sem("xt_done"), sem("xth_ready"), sem("xtl_ready")
        gm_ready, gmt_done, gmth_ready, gmtl_ready = sem("gm_ready"), sem("gmt_done"), sem("gmth_ready"), sem("gmtl_ready")
        l1_done, route1, gap1_ready, exp1_ready = sem("l1_done"), sem("route1"), sem("gap1_ready"), sem("exp1_ready")
        gh_ready, ght_done, ghth_ready, ghtl_ready = sem("gh_ready"), sem("ght_done"), sem("ghth_ready"), sem("ghtl_ready")
        out_done, out_saved, half_saved, gate1 = sem("out_done"), sem("out_saved"), sem("half_saved"), sem("gate1")
        stored = [sem(f"stored{k}") for k in range(3)]

        bank_a, bank_y, bank_mid = bank[0:2], bank[2:4], bank[4]
        slots = [(bank[0], bank[1]), (bank[2], bank[3]), (bank[4], bank[5])]
        bank_g, bank_x = bank[6], bank[7]

        block = ctx.enter_context(nc.Block())

        @block.sync
        def _(sp):
            sp.dma_start(id_b[:, :], session_ids.partition_broadcast(P)).then_inc(lens_in, 16)
            sp.dma_start(cc_b[:, :], channel_counts.partition_broadcast(P)).then_inc(lens_in, 16)
            sp.dma_start(sl_b[:, :], seq_lens.partition_broadcast(P)).then_inc(lens_in, 16)
            sp.dma_start(w_sess[:, :, :], W_sess.rearrange("(j s) c h -> (s c) j h", j=2)).then_inc(sess_in, 16)
            sp.dma_start(routers[0:K0, :], A0.rearrange("e r t -> (e r) t")).then_inc(routers_in, 16)
            sp.dma_start(routers[K0:NM, :], Wr0).then_inc(routers_in, 16)
            sp.dma_start(routers[NM:NM + E1, :], Wr1).then_inc(routers_in, 16)

            def load(t):
                if not t.real:
                    return
                if t.after(2):
                    sp.wait_ge(xl_ready, t.count(1, -1))
                sp.dma_start(xn[:, t.slot, :], x_tiles[:, ds(t.count(), 1), :].squeeze(1)).then_inc(x1_in[t.slot], 16)

            run_tiles(sp, 2, NT, 0, NT - 1, load)

            def load2(t):
                if not t.real:
                    return
                if t.after(3):
                    sp.wait_ge(xt_done, t.count(1, -2))
                sp.dma_start(xs[:, t.slot, :], x_tiles[:, ds(t.count(), 1), :].squeeze(1)).then_inc(x2_in[t.slot], 16)

            def store(t):
                if not t.real:
                    return
                sp.wait_ge(out_saved, t.count(1, 1))
                sp.dma_start(out_tiles[:, ds(t.count(), 1), :].squeeze(1), o_sb[:, t.slot, :]).then_inc(stored[t.slot], 16)

            def step(t):
                load2(t + 2)
                store(t - 2)

            run_tiles(sp, 3, NT, -2, NT + 1, step)
            for k in range(3):
                sp.wait_ge(stored[k], 16 * len(range(k, NT, 3)))

        @block.gpsimd
        def _(pool):
            g = nc.gpsimd
            g.memset(ident[:, :], 0.0).then_inc(zeroed, 1)
            g.memset(delta[:, :], 0.0).then_inc(zeroed, 1)
            g.memset(quad[:, :], 1.0).then_inc(zeroed, 1)
            g.iota(p_col[:, :], pattern=[[0, 1]], base=0, channel_multiplier=1,
                   allow_small_or_imprecise_dtypes=True).then_inc(consts, 1)
            g.iota(t_col[:, :], pattern=[[P, NC]], base=0, channel_multiplier=1,
                   allow_small_or_imprecise_dtypes=True).then_inc(consts, 1)
            g.iota(rev0[:, :], pattern=[[-1, E0]], base=E0, channel_multiplier=0,
                   allow_small_or_imprecise_dtypes=True).then_inc(consts, 1)
            g.iota(rev1[:, :], pattern=[[-1, E1]], base=E1, channel_multiplier=0,
                   allow_small_or_imprecise_dtypes=True).then_inc(consts, 1)
            g.iota(lane1[:, :], pattern=[[1, E1]], base=0, channel_multiplier=0,
                   allow_small_or_imprecise_dtypes=True).then_inc(consts, 1)
            pool.wait_ge(zeroed, 3)
            for q in range(QB):
                g.affine_select(out=delta[:, :], in_=delta[:, :], compare_op=ALU.not_equal, fill=1.0,
                                base=-C * q, pattern=[[-1, C]], channel_multiplier=1).then_inc(zeroed, 1)
                pool.wait_ge(zeroed, 4 + q)
            g.affine_select(out=quad[:, :], in_=quad[:, :], compare_op=ALU.is_ge, fill=0.0,
                            base=0, pattern=[[-C, QB]], channel_multiplier=1).then_inc(zeroed, 1)
            pool.wait_ge(zeroed, 4 + QB)
            g.affine_select(out=quad[:, :], in_=quad[:, :], compare_op=ALU.is_ge, fill=0.0,
                            base=C - 1, pattern=[[C, QB]], channel_multiplier=-1).then_inc(zeroed, 1)
            g.affine_select(out=ident[:, :], in_=ident[:, :], compare_op=ALU.not_equal, fill=1.0,
                            base=0, pattern=[[-1, P]], channel_multiplier=1).then_inc(ident_ready, 1)
            g.memset(w2_blk[:, :], 0.0).then_inc(zeroed, 1)
            g.memset(enc[:, :], 0.0).then_inc(zeroed, 1)
            g.memset(wsum[:, :, :], 0.0).then_inc(zeroed, 1)
            pool.wait_ge(zeroed, 8 + QB)
            pool.dma_start(w2_blk[0:H, 0:C], W2).then_inc(w2_in, 16)
            pool.dma_start(w2_blk[H:2 * H, C:2 * C], W2).then_inc(w2_in, 16)
            pool.dma_start(enc[0:R0, :], enc0).then_inc(enc_in, 16)
            pool.dma_start(enc[R0:RE, :], enc1).then_inc(enc_in, 16)
            pool.wait_ge(b0_in, 16 * NC)
            for k in range(2):
                g.tensor_scalar(b0_dup[:, :, k, :], b0_t[:, :, :], SCALE0, None, ALU.mult).then_inc(b_scaled, 1)
            pool.wait_ge(b1_in, 16 * NC)
            g.tensor_scalar(b1_scaled[:, :, :], b1_t[:, :, :], SCALE1, None, ALU.mult).then_inc(b_scaled, 1)

            def split_x(t):
                if not t.real:
                    return
                if t.after(2):
                    pool.wait_ge(a_done, t.count(2, -2))
                pool.wait_ge(x1_in[t.slot], t.round(16, 16))
                if t.n is None and t.c == 0:
                    pool.wait_ge(wsel_split, 4)
                shape = [P, QB, H]
                on = quad[:, :].unsqueeze(2).to_broadcast(shape)
                for dst, src in ((wbh[t.slot], w_selh[:, :, :].bitcast(fp32)), (wbl[t.slot], w_sell[:, :, :])):
                    g.tensor_tensor(dst[:, :, :], src[:, ds(t.count(), 1), :].to_broadcast(shape), on,
                                    ALU.mult).then_inc(wb_ready, 1)
                g.tensor_copy(xh[t.slot][:, :], xn[:, t.slot, :]).then_inc(xh_ready, 1)

            def mask_y(t):
                if not t.real:
                    return
                pool.wait_ge(ysum_ready, t.count(1, 1))
                if t.after(2):
                    pool.wait_ge(mid_done, t.count(1, -1))
                g.tensor_tensor(y0[:, t.slot, :, :, :], ysum[:, t.slot, :, :, :],
                                t_mask[:, :, ds(t.count(QB), QB)].unsqueeze(3).to_broadcast([P, NC, QB, C]),
                                ALU.mult).then_inc(y0_ready, 1)

            def step(t):
                split_x(t + 1)
                mask_y(t - 1)

            run_tiles(pool, 2, NT, -1, NT + 1, step)

            for d in range(NC):
                pool.wait_ge(mx_ready, d + 1)
                g.tensor_copy(mxh[:, d, :], mx[:, d, :]).then_inc(mxh_ready, 1)

        @block.scalar
        def _(act):
            a = nc.scalar
            act.dma_start(b_sess2[:, 0, :], b_sess).then_inc(bsess_in, 16)
            act.dma_start(b_sess2[:, 1, :], b_sess).then_inc(bsess_in, 16)
            act.dma_start(b2_b[:, :], b2.partition_broadcast(P)).then_inc(b2_in, 16)
            for e in range(NE):
                act.dma_start(coef[:, e, :, 0:R0], coefs0[e].rearrange("(k p) r -> p k r", p=P)).then_inc(coef_in, 16)
                act.dma_start(coef[:, e, :, R0:RE], coefs1[e].rearrange("(k p) r -> p k r", p=P)).then_inc(coef_in, 16)
                act.dma_start(mask[:, e, :, 0:R0], mask0[e].rearrange("(k p) r -> p k r", p=P)).then_inc(coef_in, 16)
                act.dma_start(mask[:, e, :, R0:RE], mask1[e].rearrange("(k p) r -> p k r", p=P)).then_inc(coef_in, 16)
            for k in range(NC):
                act.dma_start(b0_t[:, k, :].rearrange("p (e r) -> p e r", e=E0),
                              B0[:, k * P:(k + 1) * P, :].rearrange("e p r -> p e r")).then_inc(b0_in, 16)
                act.dma_start(b1_t[:, k, :].rearrange("p (e r) -> p e r", e=E1),
                              B1[:, k * P:(k + 1) * P, :].rearrange("e p r -> p e r")).then_inc(b1_in, 16)
            act.dma_start(dft_sb[:, :, :], dft.rearrange("(k p) n -> p k n", p=P)).then_inc(dft_in, 16)
            act.dma_start(wbase_nat[:, :, :], W_base.rearrange("(k p) n -> p k n", p=P)).then_inc(wbase_in, 16)
            act.dma_start(w_nat[:, :, :], W.rearrange("(k p) n -> p k n", p=P)).then_inc(w_in, 16)
            act.dma_start(a1_nat[:, :], A1.rearrange("e r d -> (e r) d")).then_inc(a1_in, 16)
            act.dma_start(bias_b[:, :], b_base.partition_broadcast(P)).then_inc(bias_in, 16)

            for k in range(2):
                act.wait_ge(wsel_done, k + 1)
                a.activation(w_sel[:, k * 8:(k + 1) * 8, :], bank[5 + k][:, :], ACT.Copy).then_inc(wsel_saved, 1)
            act.wait_ge(hbias_done, 1)
            for k in range(2):
                a.activation(h_bias[k * H:(k + 1) * H, :], bank[7][k * H:(k + 1) * H, k:NB:2],
                             ACT.Copy).then_inc(hbias_saved, 1)
            act.wait_ge(hbias_saved, 2)

            def gelu(t):
                if not t.real:
                    return
                for j in range(2):
                    act.wait_ge(a_done, t.count(2, j + 1))
                    if t.after(2) and j == 0:
                        act.wait_ge(y_done, t.count(1, -1))
                    a.activation(hact[:, t.slot, j, :], bank_a[j][:, :], ACT.Gelu,
                                 bias=h_bias[:, ds(t.count(2, j), 1)]).then_inc(h_ready, 1)

            run_tiles(act, 2, NT, 0, NT - 1, gelu)

            act.wait_ge(g_done, 1)
            a.activation(g_t[:, :], bank[5][:, :], ACT.Copy).then_inc(g_saved, 1)
            act.wait_ge(gap0_ready, 1)
            a.activation(s0[5][:, :], s0[4][:, :], ACT.Exp).then_inc(exp0_ready, 1)
            for m in range(NC):
                act.wait_ge(wb_done, m + 1)
                a.activation(wb_t[:, m, :], bank[6 + m % 2][:, :], ACT.Copy).then_inc(wb_saved, 1)
            act.wait_ge(a1t_done, 1)
            a.activation(mx[:, :, 0:K1], bank[5][:, :].rearrange("p (k n) -> p k n", k=NC), ACT.Copy).then_inc(a1t_saved, 1)
            for d in range(NC):
                act.wait_ge(m1_done, d + 1)
                a.activation(mx[:, d, L1C:NX], bank[d][:, :], ACT.Copy).then_inc(m1_saved, 1)
            act.wait_ge(m2_done, 1)
            a.activation(m2h[:, :], bank[4][:, :], ACT.Copy).then_inc(m2h_ready, 1)
            for k in range(2):
                act.wait_ge(bm_done, k + 1)
                a.activation(bmh[:, k * HX:(k + 1) * HX], bank[5 + k][:, 0:HX], ACT.Copy).then_inc(bmh_ready, 1)

            def step(t):
                u = t - 1
                if u.real:
                    act.wait_ge(gap1_ready, u.count(1, 1))
                    a.activation(s1[3][:, :], s1[2][:, :], ACT.Exp).then_inc(exp1_ready, 1)
                u = t + 1
                if u.real:
                    act.wait_ge(xt_done, u.count(1, 1))
                    if u.after(3):
                        act.wait_ge(l1_done, u.count(1, -2))
                    a.activation(xth[u.slot][:, :, :], bank_x[:, :].rearrange("p (k n) -> p k n", k=NC),
                                 ACT.Copy).then_inc(xth_ready, 1)
                u = t - 1
                if u.real:
                    act.wait_ge(ght_done, u.count(1, 1))
                    if u.after(3):
                        act.wait_ge(out_done, u.count(1, -2))
                    a.activation(ght_h[u.slot][:, :], bank_g[:, 0:P], ACT.Copy).then_inc(ghth_ready, 1)
                u = t + 1
                if u.real:
                    act.wait_ge(gmt_done, u.count(1, 1))
                    a.activation(gmt[u.slot][:, :], bank_g[:, P:2 * P], ACT.Copy).then_inc(gmth_ready, 1)

            run_tiles(act, 3, NT, -1, NT + 1, step)

        @block.vector
        def _(dve):
            v = nc.vector
            dve.wait_ge(consts, 5)
            v.tensor_scalar(quad_tmp[:, 0:1], p_col[:, :], float(C), None, ALU.is_ge).then_inc(prep, 1)
            dve.wait_ge(prep, 1)
            for q in range(2, QB):
                src, dst = (quad_tmp[:, q % 2:q % 2 + 1], quad_tmp[:, (q + 1) % 2:(q + 1) % 2 + 1])
                if q == QB - 1:
                    dst = quad_no[:, :]
                v.scalar_tensor_tensor(dst, p_col[:, :], float(C * q), src, ALU.is_ge, ALU.add).then_inc(prep, 1)
                dve.wait_ge(prep, q)
            v.scalar_tensor_tensor(in_quad[:, :], quad_no[:, :], -float(C), p_col[:, :], ALU.mult, ALU.add).then_inc(prep, 1)
            dve.wait_ge(lens_in, 48)
            for j in range(2):
                v.tensor_scalar(id_eq[:, j, :], id_b[:, :], -float(j * S // 2), quad_no[:, :], ALU.add,
                                ALU.is_equal).then_inc(prep, 1)
            dve.wait_ge(prep, QB + 2)
            for j in range(2):
                v.scalar_tensor_tensor(id_sel[:, j, :], cc_b[:, :], in_quad[:, :], id_eq[:, j, :], ALU.is_gt,
                                       ALU.mult).then_inc(prep, 1)
            dve.wait_ge(prep, QB + 4)
            dve.wait_ge(zeroed, 5 + QB)
            for k in range(4):
                n = NB // 2
                v.tensor_tensor(select[:, k * n:(k + 1) * n, :],
                                id_sel[:, :, :].rearrange("p j b -> p (j b)")[:, k * n:(k + 1) * n].unsqueeze(2).to_broadcast([P, n, C]),
                                delta[:, :].unsqueeze(1).to_broadcast([P, n, C]), ALU.mult).then_inc(select_ready, 1)
            v.tensor_scalar(one_hot[:, :], id_b[0:S, :], p_col[0:S, :], None, ALU.is_equal).then_inc(bias_hot, 1)
            for k in range(NC):
                v.tensor_scalar(t_mask[:, k, :], sl_b[:, :], t_col[:, k:k + 1], None, ALU.is_gt).then_inc(prep, 1)
            dve.wait_ge(coef_in, 64 * NE)
            v.tensor_tensor(coef[:, :, :, :].rearrange("p e k r -> p (e k r)"), coef[:, :, :, :].rearrange("p e k r -> p (e k r)"),
                            mask[:, :, :, :].rearrange("p e k r -> p (e k r)"), ALU.mult).then_inc(wsum_step, 1)
            dve.wait_ge(wsum_step, 1)
            dve.wait_ge(zeroed, 8 + QB)
            v.tensor_tensor(wsum[:, :, 0:RE], coef[:, 0, :, :], coef[:, 1, :, :], ALU.add).then_inc(wsum_step, 1)
            for e in range(2, NE):
                dve.wait_ge(wsum_step, e)
                v.tensor_tensor(wsum[:, :, 0:RE], wsum[:, :, 0:RE], coef[:, e, :, :], ALU.add).then_inc(wsum_step, 1)
            for k in range(2):
                dve.wait_ge(wsel_saved, k + 1)
                v.tensor_copy(w_selh[:, k * 8:(k + 1) * 8, :], w_sel[:, k * 8:(k + 1) * 8, :]).then_inc(wsel_split, 1)
            dve.wait_ge(wsel_split, 2)
            for k in range(2):
                v.tensor_tensor(w_sell[:, k * 8:(k + 1) * 8, :], w_sel[:, k * 8:(k + 1) * 8, :],
                                w_selh[:, k * 8:(k + 1) * 8, :].bitcast(fp32), ALU.subtract).then_inc(wsel_split, 1)
            dve.wait_ge(routers_done, 1)
            v.tensor_copy(routersT[:, :, :], bank_mid[:, 0:NC * (NM + E1)].rearrange("p (k n) -> p k n", k=NC)).then_inc(routersT_saved, 1)
            for q in range(QB):
                v.tensor_copy(id_tok[q * C:(q + 1) * C, :], id_b[q * C:(q + 1) * C, q:NB:QB]).then_inc(prep, 1)
            dve.wait_ge(prep, 2 * QB + 4 + NC)
            dve.wait_ge(b2_in, 16)
            v.tensor_tensor(lang[:, :, :], id_tok[:, :].unsqueeze(2).to_broadcast([P, NT, E1]),
                            lane1[:, :].unsqueeze(1).to_broadcast([P, NT, E1]), ALU.is_equal).then_inc(prep, 1)
            dve.wait_ge(prep, 2 * QB + 4 + NC + 1)
            v.tensor_scalar(lang[:, :, :], lang[:, :, :], LANG_BIAS, None, ALU.mult).then_inc(prep, 1)

            def step(t):
                u = t + 1
                if u.real:
                    dve.wait_ge(xh_ready, u.count(1, 1))
                    v.tensor_tensor(xl[u.slot][:, :], xn[:, u.slot, :], xh[u.slot][:, :].bitcast(fp32),
                                    ALU.subtract).then_inc(xl_ready, 1)
                u = t - 1
                if u.real:
                    dve.wait_ge(y_done, u.count(1, 1))
                    if u.after(2):
                        dve.wait_ge(y0_ready, u.count(1, -1))
                    v.tensor_tensor(ysum[:, u.slot, :, :, :].rearrange("p k b c -> p (k b) c"),
                                    bank_y[u.slot][:, :].rearrange("p (n c) -> p n c", c=C),
                                    b2_b[:, :].unsqueeze(1).to_broadcast([P, NC * QB, C]), ALU.add).then_inc(ysum_ready, 1)
                u = t - 2
                if u.real:
                    dve.wait_ge(mid_done, u.count(1, 1))
                    v.tensor_copy(mid[:, ds(u.count(), 1), :].squeeze(1), bank_mid[:, 0:NM]).then_inc(mid_saved, 1)

            run_tiles(dve, 2, NT, -1, NT + 1, step)

            done = [0]

            def then(ins, s):
                done[0] += 1
                ins.then_inc(s, 1)
                dve.wait_ge(s, done[0])

            dve.wait_ge(mid_saved, NT)
            logits = mid[:, :, K0:NM]
            wide = [P, NT, E0]
            rev = rev0[:, :].unsqueeze(1).to_broadcast(wide)

            def over(s):
                return s[:, :].unsqueeze(2).to_broadcast(wide)

            def first_max(values, top, eq, ranked, best, hot):
                then(v.tensor_reduce(top[:, :], values, X, ALU.max), route0)
                then(v.tensor_tensor(eq[:, :, :], values, over(top), ALU.is_equal), route0)
                then(v.tensor_tensor(ranked[:, :, :], eq[:, :, :], rev, ALU.mult), route0)
                then(v.tensor_reduce(best[:, :], ranked[:, :, :], X, ALU.max), route0)
                then(v.tensor_tensor(hot[:, :, :], ranked[:, :, :], over(best), ALU.is_equal), route0)

            first_max(logits, s0[0], r0[0], r0[1], s0[1], r0[2])
            then(v.scalar_tensor_tensor(r0[3][:, :, :], r0[2][:, :, :], NEG, logits, ALU.mult, ALU.add), route0)
            first_max(r0[3][:, :, :], s0[2], r0[0], r0[1], s0[3], r0[4])
            v.tensor_tensor(s0[4][:, :], s0[2][:, :], s0[0][:, :], ALU.subtract).then_inc(gap0_ready, 1)
            dve.wait_ge(exp0_ready, 1)
            then(v.tensor_scalar(s0[6][:, :], s0[5][:, :], 1.0, None, ALU.add), route0)
            then(v.reciprocal(s0[7][:, :], s0[6][:, :]), route0)
            then(v.tensor_tensor(s0[6][:, :], s0[5][:, :], s0[7][:, :], ALU.mult), route0)
            then(v.tensor_tensor(r0[5][:, :, :], r0[2][:, :, :], over(s0[7]), ALU.mult), route0)
            then(v.tensor_tensor(r0[6][:, :, :], r0[4][:, :, :], over(s0[6]), ALU.mult), route0)
            v.tensor_tensor(gates0[:, :, :], r0[5][:, :, :], r0[6][:, :, :], ALU.add).then_inc(gates0_ready, 1)

            v.tensor_copy(mx[:, :, K1:L1C], routersT[:, :, NM:NM + E1]).then_inc(wr1_saved, 1)
            dve.wait_ge(a1t_saved, 1)
            dve.wait_ge(wr1_saved, 1)
            for d in range(NC):
                dve.wait_ge(m1_saved, d + 1)
                diag = mx[:, d, L1C + d * P:L1C + (d + 1) * P]
                v.tensor_tensor(diag, diag, ident[:, :], ALU.add).then_inc(mx_ready, 1)
            for d in range(NC):
                dve.wait_ge(mxh_ready, d + 1)
                v.tensor_tensor(mxl[:, d, :], mx[:, d, :], mxh[:, d, :].bitcast(fp32), ALU.subtract).then_inc(mxl_ready, 1)
            dve.wait_ge(m2h_ready, 1)
            v.tensor_tensor(m2l[:, :], bank[4][:, :], m2h[:, :].bitcast(fp32), ALU.subtract).then_inc(m2l_ready, 1)
            for k in range(2):
                dve.wait_ge(bmh_ready, k + 1)
                v.tensor_tensor(bml[:, k * HX:(k + 1) * HX], bank[5 + k][:, 0:HX],
                                bmh[:, k * HX:(k + 1) * HX].bitcast(fp32), ALU.subtract).then_inc(bml_ready, 1)
            dve.wait_ge(gates0_ready, 1)
            dve.wait_ge(bias_in, 16)

            ROUTE1 = 11

            def route(t):
                dve.wait_ge(l1_done, t.count(1, 1))
                bank_1 = slots[t.slot][0]
                n = [0]

                def then1(ins):
                    n[0] += 1
                    ins.then_inc(route1, 1)
                    dve.wait_ge(route1, t.count(ROUTE1, n[0]))

                l, w, hot1, l2, w2_, hot2, gate = (r1[k][:, :] for k in range(7))
                top, best, gap, ex, den, g1, g2, top2, best2 = (s1[k][:, :] for k in range(9))
                then1(v.tensor_tensor(l, bank_1[:, K1:L1C], lang[:, ds(t.count(), 1), :].squeeze(1), ALU.add))
                then1(v.tensor_reduce(top, l, X, ALU.max))
                then1(v.scalar_tensor_tensor(w, l, top, rev1[:, :], ALU.is_equal, ALU.mult))
                then1(v.tensor_reduce(best, w, X, ALU.max))
                then1(v.tensor_scalar(hot1, w, best, None, ALU.is_equal))
                then1(v.scalar_tensor_tensor(l2, hot1, NEG, l, ALU.mult, ALU.add))
                then1(v.tensor_reduce(top2, l2, X, ALU.max))
                v.tensor_tensor(gap, top2, top, ALU.subtract).then_inc(gap1_ready, 1)
                v.scalar_tensor_tensor(w2_, l2, top2, rev1[:, :], ALU.is_equal, ALU.mult).then_inc(route1, 1)
                dve.wait_ge(exp1_ready, t.count(1, 1))
                v.tensor_scalar(den, ex, 1.0, None, ALU.add).then_inc(route1, 1)
                n[0] += 2
                dve.wait_ge(route1, t.count(ROUTE1, n[0]))
                v.tensor_reduce(best2, w2_, X, ALU.max).then_inc(route1, 1)
                v.reciprocal(g1, den).then_inc(route1, 1)
                n[0] += 2
                assert n[0] == ROUTE1
                dve.wait_ge(route1, t.count(ROUTE1, n[0]))
                m = [0]

                def then2(ins):
                    m[0] += 1
                    ins.then_inc(gate1, 1)
                    dve.wait_ge(gate1, t.count(3, m[0]))

                then2(v.tensor_tensor(g2, ex, g1, ALU.mult))
                then2(v.tensor_scalar(hot2, w2_, best2, g2, ALU.is_equal, ALU.mult))
                then2(v.scalar_tensor_tensor(gate, hot1, g1, hot2, ALU.mult, ALU.add))
                if t.after(3):
                    dve.wait_ge(ght_done, t.count(1, -2))
                v.tensor_tensor(gh[:, t.slot, :].rearrange("p (e r) -> p e r", e=E1),
                                bank_1[:, 0:K1].rearrange("p (e r) -> p e r", e=E1),
                                gate.unsqueeze(2).to_broadcast([P, E1, R]), ALU.mult).then_inc(gh_ready, 1)

            def step2(t):
                u = t - 1
                if u.real:
                    route(u)
                u = t + 1
                if u.real:
                    dve.wait_ge(xth_ready, u.count(1, 1))
                    v.tensor_tensor(xtl[u.slot][:, :, :], bank_x[:, :].rearrange("p (k n) -> p k n", k=NC),
                                    xth[u.slot][:, :, :].bitcast(fp32), ALU.subtract).then_inc(xtl_ready, 1)
                    if u.after(3):
                        dve.wait_ge(gmt_done, u.count(1, -2))
                    shape = [P, 2, E0, R]
                    v.tensor_tensor(gm[:, u.slot, :, :].rearrange("p a (e r) -> p a e r", e=E0),
                                    mid[:, ds(u.count(), 1), 0:K0].rearrange("p a (e r) -> p a e r", e=E0).to_broadcast(shape),
                                    gates0[:, ds(u.count(), 1), :].unsqueeze(3).to_broadcast(shape),
                                    ALU.mult).then_inc(gm_ready, 1)
                u = t - 2
                if u.real:
                    dve.wait_ge(out_done, u.count(1, 1))
                    if u.after(3):
                        dve.wait_ge(stored[u.slot], u.round(16))
                    b_0, b_1 = slots[u.slot]
                    v.tensor_tensor(o_sb[:, u.slot, 0:OA], b_0[:, L1C:HX], bias_b[:, 0:OA], ALU.add).then_inc(half_saved, 1)
                    v.tensor_tensor(o_sb[:, u.slot, OA:D], b_1[:, 0:HX], bias_b[:, OA:D], ALU.add).then_inc(out_saved, 1)
                u = t - 1
                if u.real:
                    dve.wait_ge(ghth_ready, u.count(1, 1))
                    v.tensor_tensor(ght_l[u.slot][:, :], bank_g[:, 0:P], ght_h[u.slot][:, :].bitcast(fp32),
                                    ALU.subtract).then_inc(ghtl_ready, 1)
                u = t + 1
                if u.real:
                    dve.wait_ge(gmth_ready, u.count(1, 1))
                    v.tensor_tensor(gmt[u.slot][K0:2 * K0, :], bank_g[K0:2 * K0, P:2 * P],
                                    gmt[u.slot][K0:2 * K0, :].bitcast(fp32), ALU.subtract).then_inc(gmtl_ready, 1)

            run_tiles(dve, 3, NT, -1, NT + 1, step2)

        @block.tensor
        def _(pe):
            mm = nc.tensor.matmul
            pe.wait_ge(sess_in, 16)
            pe.wait_ge(select_ready, 4)
            for t in range(NT):
                for j in range(2):
                    last = mm(bank[5 + t // 8][:, (t % 8) * H:(t % 8 + 1) * H],
                              select[:, j * NB + t * QB:j * NB + (t + 1) * QB, :].rearrange("p b c -> p (b c)"),
                              w_sess[:, j, :], start=(j == 0), stop=(j == 1))
                if t % 8 == 7:
                    last.then_inc(wsel_done, 1)
            pe.wait_ge(bsess_in, 32)
            pe.wait_ge(bias_hot, 1)
            mm(bank[7][:, 0:NB], b_sess2[:, :, :].rearrange("s a h -> s (a h)"), one_hot[:, :],
               start=True, stop=True).then_inc(hbias_done, 1)
            pe.wait_ge(routers_in, 48)
            pe.wait_ge(ident_ready, 1)
            n = NM + E1
            for k in range(NC):
                last = nc.tensor.transpose(bank_mid[:, k * n:(k + 1) * n], routers[:, k * P:(k + 1) * P], ident[0:n, 0:n])
            last.then_inc(routers_done, 1)
            pe.wait_ge(w2_in, 32)
            pe.wait_ge(routersT_saved, 1)

            def step(t):
                u = t
                if u.real:
                    pe.wait_ge(xl_ready, u.count(1, 1))
                    pe.wait_ge(wb_ready, u.count(2, 2))
                    for j in range(2):
                        wh = wbh[u.slot][:, 2 * j:2 * j + 2, :].rearrange("p b h -> p (b h)")
                        wl = wbl[u.slot][:, 2 * j:2 * j + 2, :].rearrange("p b h -> p (b h)")
                        if u.after(1):
                            pe.wait_ge(h_ready, u.count(2, j - 1))
                        mm(bank_a[j][:, :], wh, xh[u.slot][:, :], start=True, stop=False)
                        mm(bank_a[j][:, :], wh, xl[u.slot][:, :], start=False, stop=False)
                        mm(bank_a[j][:, :], wl, xh[u.slot][:, :], start=False, stop=True).then_inc(a_done, 1)
                u = t - 1
                if u.real:
                    if u.after(2):
                        pe.wait_ge(ysum_ready, u.count(1, -1))
                    for j in range(2):
                        pe.wait_ge(h_ready, u.count(2, j + 1))
                        for k in range(NC):
                            last = mm(bank_y[u.slot][:, k * P + j * 2 * C:k * P + (j + 1) * 2 * C],
                                      hact[:, u.slot, j, k * P:(k + 1) * P], w2_blk[:, :], start=True, stop=True)
                    last.then_inc(y_done, 1)
                u = t - 2
                if u.real:
                    pe.wait_ge(y0_ready, u.count(1, 1))
                    if u.after(1):
                        pe.wait_ge(mid_saved, u.count())
                    for k in range(NC):
                        last = mm(bank_mid[:, 0:NM], y0[:, u.slot, k, :, :].rearrange("p b c -> p (b c)"),
                                  routersT[:, k, 0:NM], start=(k == 0), stop=(k == NC - 1))
                    last.then_inc(mid_done, 1)

            run_tiles(pe, 2, NT, 0, NT + 1, step)

            pe.wait_ge(dft_in, 16)
            pe.wait_ge(wsum_step, NE)
            for k in range(NC):
                last = mm(bank[5][:, :], wsum[:, k, :], dft_sb[:, k, :], start=(k == 0), stop=(k == NC - 1))
            last.then_inc(g_done, 1)
            pe.wait_ge(wbase_in, 16)
            pe.wait_ge(enc_in, 32)
            pe.wait_ge(g_saved, 1)
            for m in range(NC):
                if m >= 2:
                    pe.wait_ge(wb_saved, m - 1)
                mm(bank[6 + m % 2][:, :], enc[:, m * P:(m + 1) * P], g_t[:, :], start=True, stop=False)
                for k in range(NC):
                    last = mm(bank[6 + m % 2][:, k * P:(k + 1) * P], wbase_nat[:, k, m * P:(m + 1) * P], ident[:, :],
                              start=False, stop=(k == NC - 1))
                last.then_inc(wb_done, 1)
            pe.wait_ge(a1_in, 16)
            for k in range(NC):
                last = nc.tensor.transpose(bank[5][:, k * P:(k + 1) * P], a1_nat[:, k * P:(k + 1) * P], ident[:, :])
            last.then_inc(a1t_done, 1)
            pe.wait_ge(w_in, 16)
            pe.wait_ge(wb_saved, NC)
            for d in range(NC):
                for m in range(NC):
                    last = mm(bank[d][:, :], w_nat[:, m, d * P:(d + 1) * P], wb_t[:, m, :], start=(m == 0), stop=(m == NC - 1))
                last.then_inc(m1_done, 1)
            pe.wait_ge(b_scaled, 3)
            pe.wait_ge(mid_saved, NT)
            for m in range(NC):
                last = mm(bank[4][:, :], b1_scaled[:, m, :], wb_t[:, m, :], start=(m == 0), stop=(m == NC - 1))
            last.then_inc(m2_done, 1)
            pe.wait_ge(mx_ready, NC)
            pe.wait_ge(a1t_saved, 1)
            for h in range(2):
                for d in range(NC):
                    last = mm(bank[5 + h][:, 0:HX], b0_dup[:, d, :, :].rearrange("p a n -> p (a n)"),
                              mx[:, d, h * HX:(h + 1) * HX], start=(d == 0), stop=(d == NC - 1))
                last.then_inc(bm_done, 1)
            pe.wait_ge(bml_ready, 2)
            pe.wait_ge(m2l_ready, 1)
            pe.wait_ge(mxl_ready, NC)

            def step2(t):
                u = t + 1
                if u.real:
                    pe.wait_ge(x2_in[u.slot], u.round(16, 16))
                    if u.after(1):
                        pe.wait_ge(xtl_ready, u.count())
                    for k in range(NC):
                        last = nc.tensor.transpose(bank_x[:, k * P:(k + 1) * P], xs[:, u.slot, k * P:(k + 1) * P], ident[:, :])
                    last.then_inc(xt_done, 1)
                u = t - 2
                if u.real:
                    pe.wait_ge(ghtl_ready, u.count(1, 1))
                    b_0, b_1 = slots[u.slot]
                    for lhs, rhs in ((ght_h, m2h), (ght_h, m2l), (ght_l, m2h)):
                        mm(b_0[:, L1C:HX], lhs[u.slot][:, :], rhs[:, 0:OA], start=False, stop=False, skip_group_check=True)
                        last = mm(b_1[:, 0:HX], lhs[u.slot][:, :], rhs[:, OA:D], start=False, stop=False, skip_group_check=True)
                    last.then_inc(out_done, 1)
                u = t
                if u.real:
                    pe.wait_ge(xtl_ready, u.count(1, 1))
                    if u.after(3):
                        pe.wait_ge(out_saved, u.count(1, -2))
                    for k in range(NC):
                        for part, (lhs, rhs) in enumerate(((xth, mxh), (xth, mxl), (xtl, mxh))):
                            for h in range(2):
                                mm(slots[u.slot][h][:, 0:HX], lhs[u.slot][:, k, :], rhs[:, k, h * HX:(h + 1) * HX],
                                   start=(k == 0 and part == 0), stop=False)
                u = t - 1
                if u.real:
                    pe.wait_ge(gh_ready, u.count(1, 1))
                    if (u + 1).real:
                        pe.wait_ge(gmtl_ready, u.count(1, 2))
                    nc.tensor.transpose(bank_g[:, 0:P], gh[:, u.slot, :], ident[:, :]).then_inc(ght_done, 1)
                u = t
                if u.real:
                    pe.wait_ge(gmtl_ready, u.count(1, 1))
                    for rhs in (bmh, bml):
                        for h in range(2):
                            last = mm(slots[u.slot][h][:, 0:HX], gmt[u.slot][:, :], rhs[:, h * HX:(h + 1) * HX],
                                      start=False, stop=(rhs is bml))
                    last.then_inc(l1_done, 1)
                u = t + 1
                if u.real:
                    pe.wait_ge(gm_ready, u.count(1, 1))
                    if u.after(2):
                        pe.wait_ge(ghtl_ready, u.count(1, -1))
                    nc.tensor.transpose(bank_g[:, P:2 * P], gm[:, u.slot, :, :].rearrange("p a n -> p (a n)"),
                                        ident[:, :]).then_inc(gmt_done, 1)

            run_tiles(pe, 3, NT, -1, NT + 1, step2)


_INS = ["x", "itok_B_0_7", "itok_B_2182_4065", "_lenS", "L0_cond_W_sess", "L0_cond_b_sess", "L0_cond_W2", "L0_cond_b2",
        "L0_ffn_A", "L0_ffn_B", "L0_ffn_Wr", "L1_cond_W", "L1_cond_Wr", "L1_cond_A", "L1_cond_B", "L1_ffn_W_base",
        "L1_ffn_b_base", "L1_ffn_enc0", "L1_ffn_enc1", "L1_ffn_coefs0", "L1_ffn_coefs1", "L1_ffn_mask0", "L1_ffn_mask1"]


def half_irfft(n):
    t = np.arange(n)
    rows = [np.full(n, 1.0 / np.sqrt(n))]
    for m in range(1, (n - 1) // 2 + 1):
        angle = 2.0 * np.pi * ((m * t) % n) / n
        rows += [np.sqrt(2.0 / n) * np.cos(angle), np.sqrt(2.0 / n) * np.sin(angle)]
    if n % 2 == 0:
        rows.append(np.where(t % 2 == 0, 1.0, -1.0) / np.sqrt(n))
    return (0.5 * np.stack(rows)).astype(np.float32)


def kernel(**inputs):
    import concourse.bacc as bacc
    from concourse.bass_utils import run_bass_kernel_spmd

    nc = bacc.Bacc("TRN2", target_bir_lowering=False, num_devices=1)
    arrays = {}
    for name in _INS:
        a = np.ascontiguousarray(inputs[name])
        arrays[f"in_{name}"] = a
    arrays["in_dft"] = half_irfft(inputs["L1_ffn_W_base"].shape[0])
    args = [nc.dram_tensor(n, a.shape, mybir.dt.from_np(a.dtype), kind="ExternalInput").ap() for n, a in arrays.items()]
    out = nc.dram_tensor("out_0", arrays["in_x"].shape, mybir.dt.float32, kind="ExternalOutput").ap()
    adaln_ffn(nc, *args, out)
    r = run_bass_kernel_spmd(nc, [arrays], core_ids=[0])
    return r.results[0]["out_0"]
```

```python
from contextlib import ExitStack

import numpy as np

import concourse.bass as bass
from concourse import mybir


class Tile:

    def __init__(self, n, c, ring, total):
        self.n, self.c, self.ring, self.total = n, c, ring, total
        self.slot = c % ring

    def __add__(self, d):
        return Tile(self.n, self.c + d, self.ring, self.total)

    def __sub__(self, d):
        return self + (-d)

    @property
    def real(self):
        return self.n is not None or 0 <= self.c < self.total

    def count(self, per_tile=1, more=0):
        if self.n is None:
            return per_tile * self.c + more
        return self.n * (per_tile * self.ring) + (per_tile * self.c + more)

    def round(self, per_round, more=0):
        if self.n is None:
            return per_round * (self.c // self.ring) + more
        return self.n * per_round + (per_round * (self.c // self.ring) + more)

    def after(self, d):
        return self.n is not None or self.c >= d


def run_tiles(eng, ring, total, first, last, body, head=None):
    head = head or 2 * ring - 1
    rounds = (total - 2 - head) // ring
    stop = head + rounds * ring
    for c in range(first, head):
        body(Tile(None, c, ring, total))
    with eng.Fori(0, rounds) as n:
        for c in range(head, head + ring):
            body(Tile(n, c, ring, total))
    for c in range(stop, last + 1):
        body(Tile(None, c, ring, total))


def adaln_ffn(nc, x, session_ids, seq_lens, channel_counts, W_sess, b_sess, W2, b2, A0, B0, Wr0,
              W, Wr1, A1, B1, W_base, b_base, enc0, enc1, coefs0, coefs1, mask0, mask1, dft, out):
    fp32, f32r = mybir.dt.float32, mybir.dt.float32r
    i32, u8 = mybir.dt.int32, mybir.dt.uint8
    ALU = mybir.AluOpType
    ACT = mybir.ActivationFunctionType
    X = mybir.AxisListType.X
    ds = bass.ds

    NB, C, T = x.shape
    S, _, H = W_sess.shape
    P = 128
    QB = P // C
    NT = NB // QB
    NC = T // P
    E0, R = A0.shape[0], A0.shape[1]
    E1 = A1.shape[0]
    D = T
    K0, K1 = E0 * R, E1 * R
    NM = K0 + E0
    R0, R1 = enc0.shape[0], enc1.shape[0]
    RE = R0 + R1
    NE = coefs0.shape[0]
    L1C = K1 + E1
    NX = L1C + D
    HX = NX // 2
    OA = HX - L1C
    LANG_BIAS, SCALE0, SCALE1, NEG = 5.0, 4.0, 2.0, -3.0e38

    WARM_UP, KEEP_UP = 12, 6

    HP = P // 2
    x_groups = x.rearrange("(g j b) c t -> (b c) g j t", j=2, b=QB // 2)
    x_tiles = x.rearrange("(g b) c t -> (b c) g t", b=QB)
    out_tiles = out.rearrange("(g b) c t -> (b c) g t", b=QB)

    ctx = ExitStack()
    with ctx:
        def sb(name, shape, dt=fp32):
            return ctx.enter_context(nc.sbuf_tensor(name, shape, dt))

        def sem(name):
            return ctx.enter_context(nc.semaphore(name))

        bank = [ctx.enter_context(nc.psum_tensor(f"bank{k}", [P, 512], fp32)) for k in range(8)]

        ident = sb("ident", [P, P])
        delta = sb("delta", [P, C])
        quad = sb("quad", [P, QB])
        p_col = sb("p_col", [P, 1])
        t_col = sb("t_col", [P, NC])
        pair = sb("pair", [P, QB // 2])
        quad_no = sb("quad_no", [P, 1])
        quad_tmp = sb("quad_tmp", [P, 2])
        in_quad = sb("in_quad", [P, 1])
        rev0 = sb("rev0", [P, E0])
        rev1 = sb("rev1", [P, E1])
        lane1 = sb("lane1", [P, E1])
        table = sb("table", [P, 2])

        id_b = sb("id_b", [P, NB], i32)
        cc_b = sb("cc_b", [P, NB], i32)
        sl_b = sb("sl_b", [P, NB], i32)
        id_tok = sb("id_tok", [P, NT])
        t_mask = sb("t_mask", [P, NC, NB])
        id_eq = sb("id_eq", [P, 2, NB])
        id_sel = sb("id_sel", [P, 2, NB])
        select = sb("select", [P, 2 * NB, C], f32r)
        one_hot = sb("one_hot", [S, NB])

        w_sess = sb("w_sess", [P, 2, H])
        w_sess2 = sb("w_sess2", [P, 2, 2, H], f32r)
        b_sess2 = sb("b_sess2", [S, 2, H])
        w_up = sb("w_up", [P, NT, 2, H])
        w_low = sb("w_low", [P, NT, H])
        h_bias = sb("h_bias", [P, NB // 2])
        w2_blk = sb("w2_blk", [P, 2 * C])
        b2_b = sb("b2_b", [P, C])
        routers = sb("routers", [NM + E1, D])
        routersT = sb("routersT", [P, NC, NM + E1])

        w_nat = sb("w_nat", [P, NC, D])
        wbase_nat = sb("wbase_nat", [P, NC, D])
        dft_sb = sb("dft_sb", [P, NC, D])
        enc = sb("enc", [P, D])
        coef = sb("coef", [P, NE * NC, RE])
        mask = sb("mask", [P, NE * NC, RE], u8)
        wsum = sb("wsum", [P, NC, P])
        g_t = sb("g_t", [P, D])
        w_h, w_l = (select[:, k * NB:(k + 1) * NB, :].rearrange("p b c -> p (b c)").rearrange("p (k n) -> p k n", k=NC)
                    for k in range(2))
        wb_h = sb("wb_h", [P, NC, D], f32r)
        wb_l = sb("wb_l", [P, NC, D], f32r)
        a1_nat = sb("a1_nat", [P, D])
        b1_t = sb("b1_t", [P, E1 * NC, R])
        b0_t = sb("b0_t", [P, E0 * NC, R])
        b0_h = sb("b0_h", [P, NC, 2, K0], f32r)
        b0_l = sb("b0_l", [P, NC, 2, K0], f32r)
        b1_h = sb("b1_h", [P, NC, K1], f32r)
        b1_l = sb("b1_l", [P, NC, K1], f32r)
        mxh = sb("mxh", [P, NC, NX], f32r)
        mxl = sb("mxl", [P, NC, NX], f32r)
        bmh = sb("bmh", [P, NX], f32r)
        bml = sb("bml", [P, NX], f32r)
        m2h = sb("m2h", [P, D], f32r)
        m2l = sb("m2l", [P, D], f32r)
        bias_b = sb("bias_b", [P, D])

        xn = sb("xn", [P, 2, 2, T])
        xg = [sb(f"xg{k}", [P, 2, T], f32r) for k in range(2)]
        wg_up = [sb(f"wg_up{k}", [P, 2, QB // 2, H], f32r) for k in range(2)]
        wg_low = [sb(f"wg_low{k}", [P, QB // 2, H], f32r) for k in range(2)]
        hact = sb("hact", [P, 2, 2, T])
        ysum = sb("ysum", [P, 2, NC, QB, C])
        y0 = sb("y0", [P, 2, NC, QB, C])
        mid = sb("mid", [P, NT, NM])

        r0 = [sb(f"r0_{k}", [P, NT, E0]) for k in range(7)]
        s0 = [sb(f"s0_{k}", [P, NT]) for k in range(8)]
        gates0 = sb("gates0", [P, NT, E0])
        lang = sb("lang", [P, NT, E1])

        xs = dft_sb
        xth = [sb(f"xth{k}", [P, NC, P], f32r) for k in range(3)]
        xtl = [sb(f"xtl{k}", [P, NC, P], f32r) for k in range(3)]
        gm = sb("gm", [P, 3, 2, K0])
        gmt = [sb(f"gmt{k}", [P, P], f32r) for k in range(3)]
        gh = sb("gh", [P, 3, K1])
        ght_h = [sb(f"ght_h{k}", [P, P], f32r) for k in range(3)]
        ght_l = [sb(f"ght_l{k}", [P, P], f32r) for k in range(3)]
        r1 = [sb(f"r1_{k}", [P, E1]) for k in range(8)]
        s1 = [sb(f"s1_{k}", [P, 1]) for k in range(9)]
        o_sb = wbase_nat

        ids_in, lens_in, sess_in, bsess_in, w2_in, b2_in = map(sem, ("ids_in", "lens_in", "sess_in", "bsess_in", "w2_in", "b2_in"))
        routers_in, coef_in, dft_in, enc_in = map(sem, ("routers_in", "coef_in", "dft_in", "enc_in"))
        wbase_in, w_in, a1_in, b1_in, b0_in, bias_in = map(sem, ("wbase_in", "w_in", "a1_in", "b1_in", "b0_in", "bias_in"))
        table_used = sem("table_used")
        zeroed, consts, ident_ready = sem("zeroed"), sem("consts"), sem("ident_ready")
        prep, bias_hot = sem("prep"), sem("bias_hot")
        select_first, select_last = sem("select_first"), sem("select_last")
        id_sel_ready = sem("id_sel_ready")
        first_doubled, rest_doubled, pair_ready = sem("first_doubled"), sem("rest_doubled"), sem("pair_ready")
        wsel_done, small_done = sem("wsel_done"), sem("small_done")
        wsess_split, wsel_saved, hbias_saved = sem("wsess_split"), sem("wsel_saved"), sem("hbias_saved")
        routersT_saved, wsum_step = sem("routersT_saved"), sem("wsum_step")
        w_h_ready, w_split, b1_split = sem("w_h_ready"), sem("w_split"), sem("b1_split")
        b0_split = [sem(f"b0_split{k}") for k in range(2)]
        wbh_saved = sem("wbh_saved")
        x1_in = [sem(f"x1_in{k}") for k in range(2)]
        xh_ready, xl_ready, wb_ready = sem("xh_ready"), sem("xl_ready"), sem("wb_ready")
        a_done, h_ready = sem("a_done"), sem("h_ready")
        y_done, ysum_ready, y0_ready = sem("y_done"), sem("ysum_ready"), sem("y0_ready")
        mid_done, mid_saved = sem("mid_done"), sem("mid_saved")
        g_done, g_saved, wb_done, wb_saved = sem("g_done"), sem("g_saved"), sem("wb_done"), sem("wb_saved")
        a1t_done, a1h_ready, a1l_ready, wr1_split = sem("a1t_done"), sem("a1h_ready"), sem("a1l_ready"), sem("wr1_split")
        m1_done, mx_ready, mxh_ready, mxl_ready = sem("m1_done"), sem("mx_ready"), sem("mxh_ready"), sem("mxl_ready")
        m2_done, m2h_ready, m2l_ready = sem("m2_done"), sem("m2h_ready"), sem("m2l_ready")
        bm_done, bmh_ready, bml_ready = sem("bm_done"), sem("bmh_ready"), sem("bml_ready")
        route0, gap0_ready, exp0_ready, gates0_ready = sem("route0"), sem("gap0_ready"), sem("exp0_ready"), sem("gates0_ready")
        x2_in = [sem(f"x2_in{k}") for k in range(3)]
        xt_done, xth_ready, xtl_ready = sem("xt_done"), sem("xth_ready"), sem("xtl_ready")
        gm_ready, gmt_done, gmth_ready, gmtl_ready = sem("gm_ready"), sem("gmt_done"), sem("gmth_ready"), sem("gmtl_ready")
        l1_done, x_done, route1, gap1_ready, exp1_ready = sem("l1_done"), sem("x_done"), sem("route1"), sem("gap1_ready"), sem("exp1_ready")
        gh_ready, ght_done, ghth_ready, ghtl_ready = sem("gh_ready"), sem("ght_done"), sem("ghth_ready"), sem("ghtl_ready")
        out_done, out_saved, half_saved, gate1 = sem("out_done"), sem("out_saved"), sem("half_saved"), sem("gate1")
        stored = [sem(f"stored{k}") for k in range(3)]

        bank_a, bank_y, bank_mid = bank[0:2], bank[2:4], bank[4]
        slots = [(bank[0], bank[1]), (bank[2], bank[3]), (bank[4], bank[5])]
        bank_g, bank_x = bank[6], bank[7]
        bank_bm = bank[5], bank[3]
        bank_wb = bank[4:8]
        bank_small, bank_g_t, bank_a1 = bank[2], bank[3], bank[5]
        psum_hbias = bank_small[:, 0:NB]
        psum_routers = bank_small[:, NB:NB + NC * (NM + E1)].rearrange("p (k n) -> p k n", k=NC)

        def select_part(engine, k):
            n = NB // 2
            return engine.tensor_tensor(
                select[:, k * n:(k + 1) * n, :],
                id_sel[:, :, :].rearrange("p j b -> p (j b)")[:, k * n:(k + 1) * n].unsqueeze(2).to_broadcast([P, n, C]),
                delta[:, :].unsqueeze(1).to_broadcast([P, n, C]), ALU.mult)

        block = ctx.enter_context(nc.Block())

        @block.sync
        def _(sp):
            def load(t):
                if not t.real:
                    return
                if t.after(2):
                    sp.wait_ge(xl_ready, t.count(2, -2))
                for half in range(2):
                    sp.dma_start(xn[half * HP:(half + 1) * HP, t.slot, :, :],
                                 x_groups[:, ds(t.count(), 1), :, :].squeeze(1)).then_inc(x1_in[t.slot], 16)

            def double_w(first, last, doubled):
                for j in range(2):
                    here, there = slice(j * HP, (j + 1) * HP), slice((1 - j) * HP, (2 - j) * HP)
                    sp.dma_start(w_up[there, first:last, j, :], w_up[here, first:last, j, :]).then_inc(doubled, 16)

            sp.dma_start(id_b[:, :], session_ids.partition_broadcast(P)).then_inc(ids_in, 16)
            sp.dma_start(cc_b[:, :], channel_counts.partition_broadcast(P)).then_inc(ids_in, 16)
            sp.dma_start(w_sess[:, :, :], W_sess.rearrange("(j s) c h -> (s c) j h", j=2)).then_inc(sess_in, 16)
            load(Tile(None, 0, 2, NT))
            sp.dma_start(b_sess2[:, :, :], b_sess.unsqueeze(1).to_broadcast([S, 2, H])).then_inc(bsess_in, 16)
            sp.dma_start(routers[0:K0, :], A0.rearrange("e r t -> (e r) t")).then_inc(routers_in, 16)
            sp.dma_start(routers[K0:NM, :], Wr0).then_inc(routers_in, 16)
            sp.dma_start(routers[NM:NM + E1, :], Wr1).then_inc(routers_in, 16)
            sp.dma_start(sl_b[:, :], seq_lens.partition_broadcast(P)).then_inc(lens_in, 16)
            sp.dma_start(b2_b[:, :], b2.partition_broadcast(P)).then_inc(b2_in, 16)
            sp.wait_ge(zeroed, 8 + QB)
            sp.dma_start(w2_blk[0:H, 0:C], W2).then_inc(w2_in, 16)
            sp.dma_start(w2_blk[H:2 * H, C:2 * C], W2).then_inc(w2_in, 16)
            sp.dma_start(enc[0:R0, :], enc0).then_inc(enc_in, 16)
            sp.dma_start(enc[R0:RE, :], enc1).then_inc(enc_in, 16)
            sp.wait_ge(wsel_saved, 3)
            double_w(0, 4, first_doubled)
            load(Tile(None, 1, 2, NT))
            sp.wait_ge(wsel_saved, 12)
            double_w(4, NT, rest_doubled)
            load(Tile(None, 2, 2, NT))
            load(Tile(None, 3, 2, NT))
            load(Tile(None, 4, 2, NT))
            sp.dma_start(a1_nat[:, :], A1.rearrange("e r d -> (e r) d")).then_inc(a1_in, 16)
            for k in range(2):
                sp.dma_start(w_nat[:, k * NC // 2:(k + 1) * NC // 2, :],
                             W.rearrange("(k p) n -> p k n", p=P)[:, k * NC // 2:(k + 1) * NC // 2, :]).then_inc(w_in, 16)
                load(Tile(None, 5 + k, 2, NT))
            sp.dma_start(b1_t[:, :, :], B1.rearrange("e (k p) r -> p (e k) r", p=P)).then_inc(b1_in, 16)
            load(Tile(None, 7, 2, NT))
            sp.dma_start(b0_t[:, :, :], B0.rearrange("e (k p) r -> p (e k) r", p=P)).then_inc(b0_in, 16)
            sp.dma_start(bias_b[:, :], b_base.partition_broadcast(P)).then_inc(bias_in, 16)
            run_tiles(sp, 2, NT, 8, NT - 1, load, head=8)

            sp.wait_ge(g_done, 1)

            def load2(t):
                if not t.real:
                    return
                if t.after(3):
                    sp.wait_ge(xt_done, t.count(1, -2))
                sp.dma_start(xs[:, t.slot, :], x_tiles[:, ds(t.count(), 1), :].squeeze(1)).then_inc(x2_in[t.slot], 16)

            def store(t):
                if not t.real:
                    return
                sp.wait_ge(half_saved, t.count(1, 1))
                if t.n is None and t.c == NT - 1:
                    sp.dma_start(out_tiles[:, t.c, 0:OA], o_sb[:, t.slot, 0:OA]).then_inc(stored[t.slot], 16)
                    sp.wait_ge(out_saved, NT)
                    sp.dma_start(out_tiles[:, t.c, OA:D], o_sb[:, t.slot, OA:D]).then_inc(stored[t.slot], 16)
                    return
                sp.wait_ge(out_saved, t.count(1, 1))
                sp.dma_start(out_tiles[:, ds(t.count(), 1), :].squeeze(1), o_sb[:, t.slot, :]).then_inc(stored[t.slot], 16)

            def step(t):
                load2(t + 2)
                store(t - 2)

            run_tiles(sp, 3, NT, -2, NT + 1, step)
            for k in range(3):
                sp.wait_ge(stored[k], 16 * (len(range(k, NT, 3)) + (k == (NT - 1) % 3)))

        @block.gpsimd
        def _(pool):
            g = nc.gpsimd
            g.memset(ident[:, :], 0.0).then_inc(zeroed, 1)
            g.memset(delta[:, :], 0.0).then_inc(zeroed, 1)
            g.memset(quad[:, :], 1.0).then_inc(zeroed, 1)
            g.iota(p_col[:, :], pattern=[[0, 1]], base=0, channel_multiplier=1,
                   allow_small_or_imprecise_dtypes=True).then_inc(consts, 1)
            g.iota(t_col[:, :], pattern=[[P, NC]], base=0, channel_multiplier=1,
                   allow_small_or_imprecise_dtypes=True).then_inc(consts, 1)
            g.iota(rev0[:, :], pattern=[[-1, E0]], base=E0, channel_multiplier=0,
                   allow_small_or_imprecise_dtypes=True).then_inc(consts, 1)
            g.iota(rev1[:, :], pattern=[[-1, E1]], base=E1, channel_multiplier=0,
                   allow_small_or_imprecise_dtypes=True).then_inc(consts, 1)
            g.iota(lane1[:, :], pattern=[[1, E1]], base=0, channel_multiplier=0,
                   allow_small_or_imprecise_dtypes=True).then_inc(consts, 1)
            pool.wait_ge(zeroed, 3)
            for q in range(QB):
                g.affine_select(out=delta[:, :], in_=delta[:, :], compare_op=ALU.not_equal, fill=1.0,
                                base=-C * q, pattern=[[-1, C]], channel_multiplier=1).then_inc(zeroed, 1)
                pool.wait_ge(zeroed, 4 + q)
            g.affine_select(out=quad[:, :], in_=quad[:, :], compare_op=ALU.is_ge, fill=0.0,
                            base=0, pattern=[[-C, QB]], channel_multiplier=1).then_inc(zeroed, 1)
            pool.wait_ge(zeroed, 4 + QB)
            g.affine_select(out=quad[:, :], in_=quad[:, :], compare_op=ALU.is_ge, fill=0.0,
                            base=C - 1, pattern=[[C, QB]], channel_multiplier=-1).then_inc(zeroed, 1)
            g.affine_select(out=ident[:, :], in_=ident[:, :], compare_op=ALU.not_equal, fill=1.0,
                            base=0, pattern=[[-1, P]], channel_multiplier=1).then_inc(ident_ready, 1)
            g.memset(w2_blk[:, :], 0.0).then_inc(zeroed, 1)
            g.memset(enc[:, :], 0.0).then_inc(zeroed, 1)
            g.memset(wsum[:, :, :], 0.0).then_inc(zeroed, 1)
            pool.wait_ge(id_sel_ready, 2)
            select_part(g, 3).then_inc(select_last, 1)

            def spread_w(t):
                if not t.real:
                    return
                if t.after(2):
                    pool.wait_ge(a_done, t.count(2, -2))
                if t.n is None and t.c == 0:
                    pool.wait_ge(pair_ready, 1)
                    pool.wait_ge(wsel_saved, 3)
                    pool.wait_ge(first_doubled, 32)
                if t.n is None and t.c == 3:
                    pool.wait_ge(wsel_saved, 12)
                    pool.wait_ge(rest_doubled, 32)
                up = [P, 2, QB // 2, H]
                g.tensor_tensor(wg_up[t.slot][:, :, :, :], w_up[:, ds(t.count(), 1), :, :].squeeze(1).unsqueeze(2).to_broadcast(up),
                                pair[:, :].unsqueeze(1).unsqueeze(3).to_broadcast(up), ALU.mult).then_inc(wb_ready, 1)
                low = [P, QB // 2, H]
                g.tensor_tensor(wg_low[t.slot][:, :, :], w_low[:, ds(t.count(), 1), :].to_broadcast(low),
                                pair[:, :].unsqueeze(2).to_broadcast(low), ALU.mult).then_inc(wb_ready, 1)

            def mask_y(t):
                if not t.real:
                    return
                pool.wait_ge(ysum_ready, t.count(1, 1))
                if t.after(2):
                    pool.wait_ge(mid_done, t.count(1, -1))
                g.tensor_tensor(y0[:, t.slot, :, :, :], ysum[:, t.slot, :, :, :],
                                t_mask[:, :, ds(t.count(QB), QB)].unsqueeze(3).to_broadcast([P, NC, QB, C]),
                                ALU.mult).then_inc(y0_ready, 1)

            def step(t):
                spread_w(t + 1)
                mask_y(t - 1)

            run_tiles(pool, 2, NT, -1, NT + 1, step)

            def gate_l0(t):
                if not t.real:
                    return
                if t.after(3):
                    pool.wait_ge(gmt_done, t.count(1, -2))
                shape = [P, 2, E0, R]
                g.tensor_tensor(gm[:, t.slot, :, :].rearrange("p a (e r) -> p a e r", e=E0),
                                mid[:, ds(t.count(), 1), 0:K0].rearrange("p a (e r) -> p a e r", e=E0).to_broadcast(shape),
                                gates0[:, ds(t.count(), 1), :].unsqueeze(3).to_broadcast(shape),
                                ALU.mult).then_inc(gm_ready, 1)

            pool.wait_ge(gates0_ready, 1)
            run_tiles(pool, 3, NT, -2, NT + 1, lambda t: gate_l0(t + 2))

        @block.scalar
        def _(act):
            a = nc.scalar
            act.wait_ge(consts, 5)
            a.activation(table[:, 0:1], p_col[:, :], ACT.Gelu).then_inc(table_used, 1)

            act.dma_start(wbase_nat[:, :, :], W_base.rearrange("(k p) n -> p k n", p=P)).then_inc(wbase_in, 16)
            for dst, src in ((coef, (coefs0, coefs1)), (mask, (mask0, mask1))):
                act.dma_start(dst[:, :, 0:R0], src[0].rearrange("e (k p) r -> p (e k) r", p=P)).then_inc(coef_in, 16)
                act.dma_start(dst[:, :, R0:RE], src[1].rearrange("e (k p) r -> p (e k) r", p=P)).then_inc(coef_in, 16)
            act.dma_start(dft_sb[:, :, :], dft.rearrange("(k p) n -> p k n", p=P)).then_inc(dft_in, 16)

            def split_x(t):
                act.wait_ge(x1_in[t.slot], t.round(32, 32))
                a.activation(xg[t.slot][:, :, :], xn[:, t.slot, :, :], ACT.Copy).then_inc(xh_ready, 1)

            def gelu(t):
                if (t + 2).real and not t.real:
                    split_x(t + 2)
                if not t.real:
                    return
                for j in range(2):
                    act.wait_ge(a_done, t.count(2, j + 1))
                    if t.after(2) and j == 0:
                        act.wait_ge(y_done, t.count(1, -1))
                    a.activation(hact[:, t.slot, j, :], bank_a[j][:, :], ACT.Gelu,
                                 bias=h_bias[:, ds(t.count(2, j), 1)]).then_inc(h_ready, 1)
                if (t + 2).real:
                    split_x(t + 2)

            def save_wsel(k):
                act.wait_ge(wsel_done, k + 1)
                four = slice(k * 4, (k + 1) * 4)
                gathered = bank[k][:, :].rearrange("p (g a h) -> p g a h", g=4, a=2)
                for j in range(2):
                    half = slice(j * HP, (j + 1) * HP)
                    a.activation(w_up[half, four, j, :], gathered[half, :, 0, :], ACT.Copy).then_inc(wsel_saved, 1)
                a.activation(w_low[:, four, :], gathered[:, :, 1, :], ACT.Copy).then_inc(wsel_saved, 1)

            split_x(Tile(None, 0, 2, NT))
            save_wsel(0)
            save_wsel(1)
            save_wsel(2)
            save_wsel(3)
            split_x(Tile(None, 1, 2, NT))
            act.wait_ge(small_done, 1)
            for k in range(2):
                a.activation(h_bias[k * H:(k + 1) * H, :], psum_hbias[k * H:(k + 1) * H, k:NB:2],
                             ACT.Copy).then_inc(hbias_saved, 1)
            act.wait_ge(hbias_saved, 2)
            act.wait_ge(g_done, 1)
            a.activation(g_t[:, :], bank_g_t[:, :], ACT.Copy).then_inc(g_saved, 1)
            gelu(Tile(None, 0, 2, NT))
            for m in range(NC):
                act.wait_ge(wb_done, m + 1)
                a.activation(wb_h[:, m, :], bank_wb[m][:, :], ACT.Copy).then_inc(wbh_saved, 1)
            gelu(Tile(None, 1, 2, NT))

            def gelu_and_w(t):
                gelu(t)
                if t.n is None and t.c >= NT - 2:
                    act.wait_ge(w_in, 32)
                    for k in range(2 * (t.c - NT + 2), 2 * (t.c - NT + 3)):
                        a.activation(w_h[:, k, :], w_nat[:, k, :], ACT.Copy).then_inc(w_h_ready, 1)

            run_tiles(act, 2, NT, 2, NT - 1, gelu_and_w)

            a.activation(table[:, 1:2], p_col[:, :], ACT.Sigmoid).then_inc(table_used, 1)

            act.wait_ge(a1t_done, 1)
            a.activation(mxh[:, :, 0:K1], bank_a1[:, :].rearrange("p (k n) -> p k n", k=NC), ACT.Copy).then_inc(a1h_ready, 1)
            act.wait_ge(gap0_ready, 1)
            a.activation(s0[5][:, :], s0[4][:, :], ACT.Sigmoid, scale=-1.0).then_inc(exp0_ready, 1)
            a.activation(s0[6][:, :], s0[4][:, :], ACT.Sigmoid).then_inc(exp0_ready, 1)
            for d in range(NC):
                act.wait_ge(mx_ready, d + 1)
                a.activation(mxh[:, d, L1C:NX], bank[d][:, :], ACT.Copy).then_inc(mxh_ready, 1)
            act.wait_ge(m2_done, 1)
            a.activation(m2h[:, :], bank[4][:, :], ACT.Copy).then_inc(m2h_ready, 1)

            def step(t):
                u = t + 1
                if u.real:
                    act.wait_ge(xt_done, u.count(1, 1))
                    if u.after(3):
                        act.wait_ge(x_done, u.count(1, -2))
                    a.activation(xth[u.slot][:, :, :], bank_x[:, :].rearrange("p (k n) -> p k n", k=NC),
                                 ACT.Copy).then_inc(xth_ready, 1)
                u = t + 1
                if u.real:
                    act.wait_ge(gmt_done, u.count(1, 1))
                    a.activation(gmt[u.slot][:, :], bank_g[:, P:2 * P], ACT.Copy).then_inc(gmth_ready, 1)
                u = t - 1
                if u.real:
                    act.wait_ge(gap1_ready, u.count(1, 1))
                    a.activation(s1[5][:, :], s1[2][:, :], ACT.Sigmoid, scale=-1.0).then_inc(exp1_ready, 1)
                    a.activation(s1[6][:, :], s1[2][:, :], ACT.Sigmoid).then_inc(exp1_ready, 1)
                u = t - 1
                if u.real:
                    act.wait_ge(ght_done, u.count(1, 1))
                    if u.after(3):
                        act.wait_ge(out_done, u.count(2, -4))
                    a.activation(ght_h[u.slot][:, :], bank_g[:, 0:P], ACT.Copy).then_inc(ghth_ready, 1)

            step(Tile(None, -1, 3, NT))
            for k in range(2):
                act.wait_ge(bm_done, k + 1)
                a.activation(bmh[:, k * HX:(k + 1) * HX], bank_bm[k][:, 0:HX], ACT.Copy).then_inc(bmh_ready, 1)
            run_tiles(act, 3, NT, 0, NT + 1, step)

        @block.vector
        def _(dve):
            v = nc.vector
            dve.wait_ge(consts, 5)
            v.tensor_scalar(quad_tmp[:, 0:1], p_col[:, :], float(C), None, ALU.is_ge).then_inc(prep, 1)
            dve.wait_ge(prep, 1)
            for q in range(2, QB):
                src, dst = (quad_tmp[:, q % 2:q % 2 + 1], quad_tmp[:, (q + 1) % 2:(q + 1) % 2 + 1])
                if q == QB - 1:
                    dst = quad_no[:, :]
                v.scalar_tensor_tensor(dst, p_col[:, :], float(C * q), src, ALU.is_ge, ALU.add).then_inc(prep, 1)
                dve.wait_ge(prep, q)
            v.scalar_tensor_tensor(in_quad[:, :], quad_no[:, :], -float(C), p_col[:, :], ALU.mult, ALU.add).then_inc(prep, 1)
            dve.wait_ge(ids_in, 32)
            for j in range(2):
                v.tensor_scalar(id_eq[:, j, :], id_b[:, :], -float(j * S // 2), quad_no[:, :], ALU.add,
                                ALU.is_equal).then_inc(prep, 1)
            dve.wait_ge(prep, QB + 2)
            for j in range(2):
                v.scalar_tensor_tensor(id_sel[:, j, :], cc_b[:, :], in_quad[:, :], id_eq[:, j, :], ALU.is_gt,
                                       ALU.mult).then_inc(id_sel_ready, 1)
            dve.wait_ge(id_sel_ready, 2)
            dve.wait_ge(zeroed, 5 + QB)
            select_part(v, 0).then_inc(select_first, 1)
            v.tensor_tensor(pair[:, :], quad[:, 0:QB // 2], quad[:, QB // 2:QB], ALU.add).then_inc(pair_ready, 1)
            dve.wait_ge(sess_in, 16)
            v.tensor_copy(w_sess2[:, :, 0, :], w_sess[:, :, :]).then_inc(wsess_split, 1)
            select_part(v, 2).then_inc(select_first, 1)
            dve.wait_ge(wsess_split, 1)
            v.tensor_tensor(w_sess2[:, :, 1, :], w_sess[:, :, :], w_sess2[:, :, 0, :].bitcast(fp32),
                            ALU.subtract).then_inc(wsess_split, 1)
            select_part(v, 1).then_inc(select_last, 1)
            v.tensor_scalar(one_hot[:, :], id_b[0:S, :], p_col[0:S, :], None, ALU.is_equal).then_inc(bias_hot, 1)

            def step(t):
                u = t + 1
                if u.real:
                    dve.wait_ge(xh_ready, u.count(1, 1))
                    for j in range(2):
                        low = slice((1 - j) * HP, (2 - j) * HP)
                        v.tensor_tensor(xg[u.slot][low, j, :], xn[low, u.slot, j, :], xg[u.slot][low, j, :].bitcast(fp32),
                                        ALU.subtract).then_inc(xl_ready, 1)
                u = t - 1
                if u.real:
                    dve.wait_ge(y_done, u.count(1, 1))
                    if u.after(2):
                        dve.wait_ge(y0_ready, u.count(1, -1))
                    v.tensor_tensor(ysum[:, u.slot, :, :, :].rearrange("p k b c -> p (k b) c"),
                                    bank_y[u.slot][:, :].rearrange("p (n c) -> p n c", c=C),
                                    b2_b[:, :].unsqueeze(1).to_broadcast([P, NC * QB, C]), ALU.add).then_inc(ysum_ready, 1)
                u = t - 2
                if u.real:
                    dve.wait_ge(mid_done, u.count(1, 1))
                    v.tensor_copy(mid[:, ds(u.count(), 1), :].squeeze(1), bank_mid[:, 0:NM]).then_inc(mid_saved, 1)

            step(Tile(None, -1, 2, NT))
            dve.wait_ge(coef_in, 64)
            v.tensor_tensor(coef[:, :, :], coef[:, :, :], mask[:, :, :], ALU.mult).then_inc(wsum_step, 1)
            dve.wait_ge(wsum_step, 1)
            dve.wait_ge(zeroed, 8 + QB)
            v.tensor_tensor(wsum[:, :, 0:RE], coef[:, 0:NC, :], coef[:, NC:2 * NC, :], ALU.add).then_inc(wsum_step, 1)
            for e in range(2, NE):
                dve.wait_ge(wsum_step, e)
                v.tensor_tensor(wsum[:, :, 0:RE], wsum[:, :, 0:RE], coef[:, e * NC:(e + 1) * NC, :], ALU.add).then_inc(wsum_step, 1)
            step(Tile(None, 0, 2, NT))
            dve.wait_ge(hbias_saved, 2)
            v.tensor_copy(routersT[:, :, :], psum_routers).then_inc(routersT_saved, 1)
            dve.wait_ge(lens_in, 16)
            for k in range(NC):
                v.tensor_scalar(t_mask[:, k, :], sl_b[:, :], t_col[:, k:k + 1], None, ALU.is_gt).then_inc(prep, 1)
            dve.wait_ge(b2_in, 16)
            step(Tile(None, 1, 2, NT))

            def wb_low(m):
                dve.wait_ge(wbh_saved, m + 1)
                v.tensor_tensor(wb_l[:, m, :], bank_wb[m][:, :], wb_h[:, m, :].bitcast(fp32), ALU.subtract).then_inc(wb_saved, 1)

            wb_low(0)

            def split_scaled(parts, src, scale, s):
                src = src[:, :, :].rearrange("p (e k) r -> p k e r", k=NC)
                high, low = (part.rearrange("p k (e r) -> p k e r", r=R) for part in parts)
                v.tensor_scalar(high, src, scale, None, ALU.mult).then_inc(s, 1)
                dve.wait_ge(s, 1)
                for k in range(NC):
                    v.scalar_tensor_tensor(low[:, k], src[:, k], scale, high[:, k].bitcast(fp32), ALU.mult,
                                           ALU.subtract).then_inc(s, 1)

            def step_and_weights(t):
                step(t)
                if t.n is None and 2 <= t.c < NC + 1:
                    wb_low(t.c - 1)
                if t.n is None and t.c in (NT - 2, NT - 1):
                    for k in range(2 * (t.c - NT + 2), 2 * (t.c - NT + 3)):
                        dve.wait_ge(w_h_ready, k + 1)
                        v.tensor_tensor(w_l[:, k, :], w_nat[:, k, :], w_h[:, k, :].bitcast(fp32), ALU.subtract).then_inc(w_split, 1)
                if t.n is None and t.c == NT - 3:
                    dve.wait_ge(b1_in, 16)
                    split_scaled((b1_h[:, :, :], b1_l[:, :, :]), b1_t, SCALE1, b1_split)
                if t.n is None and t.c == NT:
                    dve.wait_ge(b0_in, 16)
                    for k in range(2):
                        split_scaled((b0_h[:, :, k, :], b0_l[:, :, k, :]), b0_t, SCALE0, b0_split[k])

            run_tiles(dve, 2, NT, 2, NT + 1, step_and_weights, head=NC + 1)

            done = [0]

            def then(ins, s):
                done[0] += 1
                ins.then_inc(s, 1)
                dve.wait_ge(s, done[0])

            dve.wait_ge(mid_saved, NT)
            logits = mid[:, :, K0:NM]
            wide = [P, NT, E0]
            rev = rev0[:, :].unsqueeze(1).to_broadcast(wide)

            def over(s):
                return s[:, :].unsqueeze(2).to_broadcast(wide)

            def first_max(values, top, eq, ranked, best, hot):
                then(v.tensor_reduce(top[:, :], values, X, ALU.max), route0)
                then(v.tensor_tensor(eq[:, :, :], values, over(top), ALU.is_equal), route0)
                then(v.tensor_tensor(ranked[:, :, :], eq[:, :, :], rev, ALU.mult), route0)
                then(v.tensor_reduce(best[:, :], ranked[:, :, :], X, ALU.max), route0)
                then(v.tensor_tensor(hot[:, :, :], ranked[:, :, :], over(best), ALU.is_equal), route0)

            first_max(logits, s0[0], r0[0], r0[1], s0[1], r0[2])
            then(v.scalar_tensor_tensor(r0[3][:, :, :], r0[2][:, :, :], NEG, logits, ALU.mult, ALU.add), route0)
            first_max(r0[3][:, :, :], s0[2], r0[0], r0[1], s0[3], r0[4])
            v.tensor_tensor(s0[4][:, :], s0[2][:, :], s0[0][:, :], ALU.subtract).then_inc(gap0_ready, 1)
            dve.wait_ge(exp0_ready, 2)
            then(v.tensor_tensor(r0[5][:, :, :], r0[2][:, :, :], over(s0[5]), ALU.mult), route0)
            then(v.tensor_tensor(r0[6][:, :, :], r0[4][:, :, :], over(s0[6]), ALU.mult), route0)
            v.tensor_tensor(gates0[:, :, :], r0[5][:, :, :], r0[6][:, :, :], ALU.add).then_inc(gates0_ready, 1)

            v.tensor_copy(mxh[:, :, K1:L1C], routersT[:, :, NM:NM + E1]).then_inc(wr1_split, 1)
            dve.wait_ge(wr1_split, 1)
            v.tensor_tensor(mxl[:, :, K1:L1C], routersT[:, :, NM:NM + E1], mxh[:, :, K1:L1C].bitcast(fp32),
                            ALU.subtract).then_inc(wr1_split, 1)
            dve.wait_ge(a1h_ready, 1)
            v.tensor_tensor(mxl[:, :, 0:K1], bank_a1[:, :].rearrange("p (k n) -> p k n", k=NC),
                            mxh[:, :, 0:K1].bitcast(fp32), ALU.subtract).then_inc(a1l_ready, 1)
            for d in range(NC + 1):
                if d < NC:
                    dve.wait_ge(m1_done, d + 1)
                    diag = bank[d][:, d * P:(d + 1) * P]
                    v.tensor_tensor(diag, diag, ident[:, :], ALU.add).then_inc(mx_ready, 1)
                if d >= 1:
                    dve.wait_ge(mxh_ready, d)
                    v.tensor_tensor(mxl[:, d - 1, L1C:NX], bank[d - 1][:, :], mxh[:, d - 1, L1C:NX].bitcast(fp32),
                                    ALU.subtract).then_inc(mxl_ready, 1)
            for q in range(QB):
                v.tensor_copy(id_tok[q * C:(q + 1) * C, :], id_b[q * C:(q + 1) * C, q:NB:QB]).then_inc(prep, 1)
            dve.wait_ge(prep, 2 * QB + 2 + NC)
            v.tensor_tensor(lang[:, :, :], id_tok[:, :].unsqueeze(2).to_broadcast([P, NT, E1]),
                            lane1[:, :].unsqueeze(1).to_broadcast([P, NT, E1]), ALU.is_equal).then_inc(prep, 1)
            dve.wait_ge(prep, 2 * QB + 3 + NC)
            v.tensor_scalar(lang[:, :, :], lang[:, :, :], LANG_BIAS, None, ALU.mult).then_inc(prep, 1)
            dve.wait_ge(m2h_ready, 1)
            v.tensor_tensor(m2l[:, :], bank[4][:, :], m2h[:, :].bitcast(fp32), ALU.subtract).then_inc(m2l_ready, 1)
            dve.wait_ge(bias_in, 16)

            ROUTE1 = 12

            l, w, hot1, l2, w2_, hot2, gate, hot2g = (r1[k][:, :] for k in range(8))
            top, best, gap, top2, best2, g1, g2 = (s1[k][:, :] for k in range(7))

            def chained(u, steps):
                if u.real:
                    dve.wait_ge(route1, u.count(ROUTE1, steps))

            def output(u, h):
                if u.real:
                    dve.wait_ge(out_done, u.count(2, h + 1))
                    if u.after(3) and h == 0:
                        dve.wait_ge(stored[u.slot], u.round(16))
                    cols, src = ((slice(0, OA), slots[u.slot][0][:, L1C:HX]), (slice(OA, D), slots[u.slot][1][:, 0:HX]))[h]
                    v.tensor_tensor(o_sb[:, u.slot, cols], src, bias_b[:, cols], ALU.add).then_inc((half_saved, out_saved)[h], 1)

            def step2(t):
                nxt, old = t + 1, t - 2
                if nxt.real:
                    dve.wait_ge(xth_ready, nxt.count(1, 1))
                    v.tensor_tensor(xtl[nxt.slot][:, :, :], bank_x[:, :].rearrange("p (k n) -> p k n", k=NC),
                                    xth[nxt.slot][:, :, :].bitcast(fp32), ALU.subtract).then_inc(xtl_ready, 1)
                u = t - 1
                chained(u, 6)
                if u.real:
                    v.tensor_reduce(top2, l2, X, ALU.max).then_inc(route1, 1)
                if nxt.real:
                    dve.wait_ge(gmth_ready, nxt.count(1, 1))
                    v.tensor_tensor(gmt[nxt.slot][K0:2 * K0, :], bank_g[K0:2 * K0, P:2 * P],
                                    gmt[nxt.slot][K0:2 * K0, :].bitcast(fp32), ALU.subtract).then_inc(gmtl_ready, 1)
                chained(u, 7)
                if u.real:
                    v.tensor_tensor(gap, top2, top, ALU.subtract).then_inc(gap1_ready, 1)
                    v.scalar_tensor_tensor(w2_, l2, top2, rev1[:, :], ALU.is_equal, ALU.mult).then_inc(route1, 1)
                if t.real:
                    output(old, 0)
                chained(u, 8)
                if u.real:
                    v.tensor_reduce(best2, w2_, X, ALU.max).then_inc(route1, 1)
                chained(u, 9)
                if u.real:
                    v.tensor_scalar(hot2, w2_, best2, None, ALU.is_equal).then_inc(route1, 1)
                if t.real:
                    output(old, 1)
                if u.real:
                    dve.wait_ge(exp1_ready, u.count(2, 2))
                chained(u, 10)
                if u.real:
                    v.tensor_scalar(hot2g, hot2, g2, None, ALU.mult).then_inc(route1, 1)
                chained(u, 11)
                if u.real:
                    v.scalar_tensor_tensor(gate, hot1, g1, hot2g, ALU.mult, ALU.add).then_inc(route1, 1)
                chained(u, 12)
                if u.real:
                    if u.after(3):
                        dve.wait_ge(ght_done, u.count(1, -2))
                    v.tensor_tensor(gh[:, u.slot, :].rearrange("p (e r) -> p e r", e=E1),
                                    slots[u.slot][0][:, 0:K1].rearrange("p (e r) -> p e r", e=E1),
                                    gate.unsqueeze(2).to_broadcast([P, E1, R]), ALU.mult).then_inc(gh_ready, 1)
                if not t.real:
                    output(old, 0)
                    output(old, 1)
                if t.real:
                    dve.wait_ge(l1_done, t.count(1, 1))
                    v.tensor_tensor(l, slots[t.slot][0][:, K1:L1C], lang[:, ds(t.count(), 1), :].squeeze(1),
                                    ALU.add).then_inc(route1, 1)
                chained(t, 1)
                if t.real:
                    v.tensor_reduce(top, l, X, ALU.max).then_inc(route1, 1)
                chained(t, 2)
                if t.real:
                    v.scalar_tensor_tensor(w, l, top, rev1[:, :], ALU.is_equal, ALU.mult).then_inc(route1, 1)
                chained(t, 3)
                if t.real:
                    v.tensor_reduce(best, w, X, ALU.max).then_inc(route1, 1)
                chained(t, 4)
                if t.real:
                    v.tensor_scalar(hot1, w, best, None, ALU.is_equal).then_inc(route1, 1)
                chained(t, 5)
                if t.real:
                    v.scalar_tensor_tensor(l2, hot1, NEG, l, ALU.mult, ALU.add).then_inc(route1, 1)
                if u.real:
                    dve.wait_ge(ghth_ready, u.count(1, 1))
                    v.tensor_tensor(ght_l[u.slot][:, :], bank_g[:, 0:P], ght_h[u.slot][:, :].bitcast(fp32),
                                    ALU.subtract).then_inc(ghtl_ready, 1)

            step2(Tile(None, -1, 3, NT))
            for k in range(2):
                dve.wait_ge(bmh_ready, k + 1)
                v.tensor_tensor(bml[:, k * HX:(k + 1) * HX], bank_bm[k][:, 0:HX],
                                bmh[:, k * HX:(k + 1) * HX].bitcast(fp32), ALU.subtract).then_inc(bml_ready, 1)
            run_tiles(dve, 3, NT, 0, NT + 1, step2)

        @block.tensor
        def _(pe):
            mm = nc.tensor.matmul
            def gather(first, last):
                for t in range(first, last):
                    for j in range(2):
                        done = mm(bank[t // 4][:, (t % 4) * 2 * H:(t % 4 + 1) * 2 * H],
                                  select[:, j * NB + t * QB:j * NB + (t + 1) * QB, :].rearrange("p b c -> p (b c)"),
                                  w_sess2[:, j, :, :].rearrange("p a h -> p (a h)"), start=(j == 0), stop=(j == 1))
                    if t % 4 == 3:
                        done.then_inc(wsel_done, 1)

            pe.wait_ge(ident_ready, 1)
            for _ in range(WARM_UP):
                mm(bank[7][:, 0:P], ident[:, :], ident[:, :], start=True, stop=True)
            pe.wait_ge(wsess_split, 2)
            pe.wait_ge(select_first, 2)
            gather(0, NT // 2)
            pe.wait_ge(select_last, 2)
            gather(NT // 2, NT)
            pe.wait_ge(wbase_in, 16)
            for m in range(NC):
                for k in range(NC):
                    mm(bank_wb[m][:, k * P:(k + 1) * P], wbase_nat[:, k, m * P:(m + 1) * P], ident[:, :],
                       start=(k == 0), stop=False)
            pe.wait_ge(bsess_in, 16)
            pe.wait_ge(bias_hot, 1)
            pe.wait_ge(wsel_saved, 9)
            mm(psum_hbias, b_sess2[:, :, :].rearrange("s a h -> s (a h)"), one_hot[:, :], start=True, stop=True)
            pe.wait_ge(routers_in, 48)
            n = NM + E1
            for k in range(NC):
                last = nc.tensor.transpose(psum_routers[:, k, :], routers[:, k * P:(k + 1) * P], ident[0:n, 0:n])
            last.then_inc(small_done, 1)
            pe.wait_ge(dft_in, 16)
            pe.wait_ge(wsum_step, NE)
            pe.wait_ge(wsel_saved, 12)
            for k in range(NC):
                last = mm(bank_g_t[:, :], wsum[:, k, :], dft_sb[:, k, :], start=(k == 0), stop=(k == NC - 1))
            last.then_inc(g_done, 1)

            def step(t):
                u = t
                if u.real:
                    pe.wait_ge(xl_ready, u.count(2, 2))
                    pe.wait_ge(wb_ready, u.count(2, 2))
                    for j in range(2):
                        up = slice(j * HP, (j + 1) * HP)
                        if u.after(1):
                            pe.wait_ge(h_ready, u.count(2, j - 1))
                        else:
                            pe.wait_ge(wsel_saved, 3 * j + 3)
                        mm(bank_a[j][:, :], wg_up[u.slot][:, j, :, :].rearrange("p b h -> p (b h)"), xg[u.slot][:, j, :],
                           start=True, stop=False)
                        mm(bank_a[j][:, :], wg_low[u.slot][up, :, :].rearrange("p b h -> p (b h)"), xg[u.slot][up, j, :],
                           start=False, stop=True).then_inc(a_done, 1)
                u = t - 1
                if u.real:
                    if u.after(2):
                        pe.wait_ge(ysum_ready, u.count(1, -1))
                    elif u.c == 0:
                        pe.wait_ge(w2_in, 32)
                        pe.wait_ge(routersT_saved, 1)
                    else:
                        pe.wait_ge(g_saved, 1)
                    for j in range(2):
                        pe.wait_ge(h_ready, u.count(2, j + 1))
                        for k in range(NC):
                            last = mm(bank_y[u.slot][:, k * P + j * 2 * C:k * P + (j + 1) * 2 * C],
                                      hact[:, u.slot, j, k * P:(k + 1) * P], w2_blk[:, :], start=True, stop=True)
                    last.then_inc(y_done, 1)
                u = t - 2
                if u.real:
                    pe.wait_ge(y0_ready, u.count(1, 1))
                    if u.after(1):
                        pe.wait_ge(mid_saved, u.count())
                    if u.n is None and u.c == 0:
                        pe.wait_ge(wb_saved, 1)
                    for k in range(NC):
                        last = mm(bank_mid[:, 0:NM], y0[:, u.slot, k, :, :].rearrange("p b c -> p (b c)"),
                                  routersT[:, k, 0:NM], start=(k == 0), stop=(k == NC - 1))
                    last.then_inc(mid_done, 1)

            step(Tile(None, 0, 2, NT))
            pe.wait_ge(enc_in, 32)
            pe.wait_ge(g_saved, 1)
            for m in range(NC):
                mm(bank_wb[m][:, :], enc[:, m * P:(m + 1) * P], g_t[:, :], start=False, stop=True).then_inc(wb_done, 1)
            step(Tile(None, 1, 2, NT))
            run_tiles(pe, 2, NT, 2, NT, step)

            pe.wait_ge(a1_in, 16)
            pe.wait_ge(wb_saved, NC)
            for k in range(NC):
                last = nc.tensor.transpose(bank_a1[:, k * P:(k + 1) * P], a1_nat[:, k * P:(k + 1) * P], ident[:, :])
            last.then_inc(a1t_done, 1)

            def split_product(dst, lhs, rhs, cols, ready=None):
                parts = [(lhs[0], rhs[0]), (lhs[0], rhs[1]), (lhs[1], rhs[0])]
                for k in range(NC):
                    if ready is not None:
                        pe.wait_ge(ready, k + 1)
                    for part, (a, b) in enumerate(parts):
                        last = mm(dst, a(k), b[:, k, cols], start=(k == 0 and part == 0), stop=(k == NC - 1 and part == 2))
                return last

            def product_m1(d):
                at = slice(d * P, (d + 1) * P)
                split_product(bank[d][:, :], [lambda k, w=w: w[:, k, at] for w in (w_h, w_l)], (wb_h, wb_l),
                              slice(0, D), w_split).then_inc(m1_done, 1)

            product_m1(0)
            step(Tile(None, NT + 1, 2, NT))
            for d in range(1, NC):
                product_m1(d)
            pe.wait_ge(b1_split, 1 + NC)
            pe.wait_ge(mid_saved, NT)
            split_product(bank[4][:, :], [lambda k, b=b: b[:, k, :] for b in (b1_h, b1_l)], (wb_h, wb_l),
                          slice(0, D)).then_inc(m2_done, 1)

            def step2(t):
                u = t + 1
                if u.real:
                    pe.wait_ge(x2_in[u.slot], u.round(16, 16))
                    if u.after(1):
                        pe.wait_ge(xtl_ready, u.count())
                    for k in range(NC):
                        last = nc.tensor.transpose(bank_x[:, k * P:(k + 1) * P], xs[:, u.slot, k * P:(k + 1) * P], ident[:, :])
                    last.then_inc(xt_done, 1)
                def older():
                    u = t + 1
                    if u.real:
                        pe.wait_ge(gm_ready, u.count(1, 1))
                        if u.after(3):
                            pe.wait_ge(ghtl_ready, u.count(1, -2))
                        elif u.after(1):
                            pe.wait_ge(gmtl_ready, u.count())
                        nc.tensor.transpose(bank_g[:, P:2 * P], gm[:, u.slot, :, :].rearrange("p a n -> p (a n)"),
                                            ident[:, :]).then_inc(gmt_done, 1)
                    u = t - 2
                    if u.real:
                        pe.wait_ge(ghtl_ready, u.count(1, 1))
                        b_0, b_1 = slots[u.slot]
                        for dst, cols in ((b_0[:, L1C:HX], slice(0, OA)), (b_1[:, 0:HX], slice(OA, D))):
                            for lhs, rhs in ((ght_h, m2h), (ght_h, m2l), (ght_l, m2h)):
                                last = mm(dst, lhs[u.slot][:, :], rhs[:, cols], start=False, stop=False, skip_group_check=True)
                            last.then_inc(out_done, 1)

                if not t.real:
                    older()
                if t.n is None and t.c == NT:
                    for _ in range(KEEP_UP):
                        mm(bank_x[:, 0:P], ident[:, :], ident[:, :], start=True, stop=True)
                u = t
                for h in range(2):
                    if u.real:
                        if h == 0:
                            pe.wait_ge(xtl_ready, u.count(1, 1))
                        if h == 0 and u.after(3):
                            pe.wait_ge(out_saved, u.count(1, -2))
                        for k in range(NC):
                            if h == 0 and k == 1:
                                older()
                            for part, (lhs, rhs) in enumerate(((xth, mxh), (xth, mxl), (xtl, mxh))):
                                mm(slots[u.slot][h][:, 0:HX], lhs[u.slot][:, k, :], rhs[:, k, h * HX:(h + 1) * HX],
                                   start=(k == 0 and part == 0), stop=False)
                    if h == 1 and (t - 1).real:
                        b = t - 1
                        pe.wait_ge(gh_ready, b.count(1, 1))
                        if (b + 2).real:
                            pe.wait_ge(gmtl_ready, b.count(1, 3))
                        nc.tensor.transpose(bank_g[:, 0:P], gh[:, b.slot, :], ident[:, :]).then_inc(ght_done, 1)
                    if u.real:
                        if h == 0:
                            pe.wait_ge(gmtl_ready, u.count(1, 1))
                        if u.n is None and u.c == 0:
                            pe.wait_ge(bml_ready, h + 1)
                            if h == 1:
                                pe.wait_ge(m2l_ready, 1)
                        for rhs in (bmh, bml):
                            last = mm(slots[u.slot][h][:, 0:HX], gmt[u.slot][:, :], rhs[:, h * HX:(h + 1) * HX],
                                      start=False, stop=(rhs is bml))
                        last.then_inc((l1_done, x_done)[h], 1)
                if t.n is None and t.c == NT:
                    for _ in range(KEEP_UP // 2):
                        mm(bank_x[:, 0:P], ident[:, :], ident[:, :], start=True, stop=True)

            step2(Tile(None, -1, 3, NT))
            for k in range(2):
                pe.wait_ge(b0_split[k], 1 + NC)
            pe.wait_ge(a1l_ready, 1)
            pe.wait_ge(wr1_split, 2)
            for h in range(2):
                split_product(bank_bm[h][:, 0:HX], [lambda k, b=b: b[:, k, :, :].rearrange("p a n -> p (a n)") for b in (b0_h, b0_l)],
                              (mxh, mxl), slice(h * HX, (h + 1) * HX), mxl_ready).then_inc(bm_done, 1)
            run_tiles(pe, 3, NT, 0, NT + 1, step2)


_INS = ["x", "itok_B_0_7", "itok_B_2182_4065", "_lenS", "L0_cond_W_sess", "L0_cond_b_sess", "L0_cond_W2", "L0_cond_b2",
        "L0_ffn_A", "L0_ffn_B", "L0_ffn_Wr", "L1_cond_W", "L1_cond_Wr", "L1_cond_A", "L1_cond_B", "L1_ffn_W_base",
        "L1_ffn_b_base", "L1_ffn_enc0", "L1_ffn_enc1", "L1_ffn_coefs0", "L1_ffn_coefs1", "L1_ffn_mask0", "L1_ffn_mask1"]


def half_irfft(n):
    t = np.arange(n)
    rows = [np.full(n, 1.0 / np.sqrt(n))]
    for m in range(1, (n - 1) // 2 + 1):
        angle = 2.0 * np.pi * ((m * t) % n) / n
        rows += [np.sqrt(2.0 / n) * np.cos(angle), np.sqrt(2.0 / n) * np.sin(angle)]
    if n % 2 == 0:
        rows.append(np.where(t % 2 == 0, 1.0, -1.0) / np.sqrt(n))
    return (0.5 * np.stack(rows)).astype(np.float32)


def kernel(**inputs):
    import concourse.bacc as bacc
    from concourse.bass_utils import run_bass_kernel_spmd

    nc = bacc.Bacc("TRN2", target_bir_lowering=False, num_devices=1)
    arrays = {}
    for name in _INS:
        a = np.ascontiguousarray(inputs[name])
        arrays[f"in_{name}"] = a
    arrays["in_dft"] = half_irfft(inputs["L1_ffn_W_base"].shape[0])
    args = [nc.dram_tensor(n, a.shape, mybir.dt.from_np(a.dtype), kind="ExternalInput").ap() for n, a in arrays.items()]
    out = nc.dram_tensor("out_0", arrays["in_x"].shape, mybir.dt.float32, kind="ExternalOutput").ap()
    adaln_ffn(nc, *args, out)
    r = run_bass_kernel_spmd(nc, [arrays], core_ids=[0])
    return r.results[0]["out_0"]
```

```python
from contextlib import ExitStack

import numpy as np

import concourse.bass as bass
from concourse import mybir


class Tile:

    def __init__(self, n, c, ring, total):
        self.n, self.c, self.ring, self.total = n, c, ring, total
        self.slot = c % ring

    def __add__(self, d):
        return Tile(self.n, self.c + d, self.ring, self.total)

    def __sub__(self, d):
        return self + (-d)

    @property
    def real(self):
        return self.n is not None or 0 <= self.c < self.total

    @property
    def last(self):
        return self.n is None and self.c == self.total - 1

    @property
    def past(self):
        return self.n is None and self.c == self.total

    def count(self, per_tile=1, more=0):
        if self.n is None:
            return per_tile * self.c + more
        return self.n * (per_tile * self.ring) + (per_tile * self.c + more)

    def round(self, per_round, more=0):
        if self.n is None:
            return per_round * (self.c // self.ring) + more
        return self.n * per_round + (per_round * (self.c // self.ring) + more)

    def after(self, d):
        return self.n is not None or self.c >= d


def run_tiles(eng, ring, total, first, last, body, head=None):
    head = head or 2 * ring - 1
    rounds = (total - 2 - head) // ring
    stop = head + rounds * ring
    for c in range(first, head):
        body(Tile(None, c, ring, total))
    with eng.Fori(0, rounds) as n:
        for c in range(head, head + ring):
            body(Tile(n, c, ring, total))
    for c in range(stop, last + 1):
        body(Tile(None, c, ring, total))


def adaln_ffn(nc, x, session_ids, seq_lens, channel_counts, W_sess, b_sess, W2, b2, A0, B0, Wr0,
              W, Wr1, A1, B1, W_base, b_base, enc0, enc1, coefs0, coefs1, mask0, mask1, dft, out):
    fp32, f32r = mybir.dt.float32, mybir.dt.float32r
    i32, u8 = mybir.dt.int32, mybir.dt.uint8
    ALU = mybir.AluOpType
    ACT = mybir.ActivationFunctionType
    X = mybir.AxisListType.X
    ds = bass.ds

    NB, C, T = x.shape
    S, _, H = W_sess.shape
    P = 128
    QB = P // C
    NT = NB // QB
    NC = T // P
    E0, R = A0.shape[0], A0.shape[1]
    E1 = A1.shape[0]
    D = T
    K0, K1 = E0 * R, E1 * R
    NM = K0 + E0
    R0, R1 = enc0.shape[0], enc1.shape[0]
    RE = R0 + R1
    NE = coefs0.shape[0]
    L1C = K1 + E1
    NX = L1C + D
    OA = D // 2
    half_x = (slice(0, L1C + OA), slice(L1C + OA, NX))
    NX0, NX1 = L1C + OA, D - OA
    LANG_BIAS, SCALE0, SCALE1, NEG = 5.0, 4.0, 2.0, -3.0e38

    WARM_UP, KEEP_UP = 5, 2

    HP = P // 2
    x_groups = x.rearrange("(g j b) c t -> (b c) g j t", j=2, b=QB // 2)
    x_tiles = x.rearrange("(g b) c t -> (b c) g t", b=QB)
    out_tiles = out.rearrange("(g b) c t -> (b c) g t", b=QB)

    ctx = ExitStack()
    with ctx:
        def sb(name, shape, dt=fp32):
            return ctx.enter_context(nc.sbuf_tensor(name, shape, dt))

        def sem(name):
            return ctx.enter_context(nc.semaphore(name))

        bank = [ctx.enter_context(nc.psum_tensor(f"bank{k}", [P, 512], fp32)) for k in range(8)]

        ident = sb("ident", [P, P])
        delta = sb("delta", [P, C])
        quad = sb("quad", [P, QB])
        p_col = sb("p_col", [P, 1])
        t_col = sb("t_col", [P, NC])
        pair = sb("pair", [P, QB // 2])
        quad_no = sb("quad_no", [P, 1])
        quad_tmp = sb("quad_tmp", [P, 2])
        in_quad = sb("in_quad", [P, 1])
        rev0 = sb("rev0", [P, E0])
        rev1 = sb("rev1", [P, E1])
        lane1 = sb("lane1", [P, E1])
        table = sb("table", [P, 2])

        id_b = sb("id_b", [P, NB], i32)
        cc_b = sb("cc_b", [P, NB], i32)
        sl_b = sb("sl_b", [P, NB], i32)
        id_tok = sb("id_tok", [P, NT])
        t_mask = sb("t_mask", [P, NC, NB])
        id_eq = sb("id_eq", [P, 2, NB])
        id_sel = sb("id_sel", [P, 2, NB])
        select = sb("select", [P, 2 * NB, C], f32r)
        one_hot = sb("one_hot", [S, NB])

        w_sess = sb("w_sess", [P, 2, H])
        w_sess2 = sb("w_sess2", [P, 2, 2, H], f32r)
        b_sess2 = sb("b_sess2", [S, 2, H])
        w_up = sb("w_up", [P, 2, NT, H])
        w_low = sb("w_low", [P, NT, H])
        h_bias = sb("h_bias", [P, NB // 2])
        w2_blk = sb("w2_blk", [P, 2 * C])
        b2_b = sb("b2_b", [P, C])
        routers = sb("routers", [NM + E1, D])
        routersT = sb("routersT", [P, NC, NM + E1])

        w_nat = sb("w_nat", [P, NC, D])
        wbase_nat = sb("wbase_nat", [P, NC, D])
        dft_sb = sb("dft_sb", [P, NC, D])
        enc = sb("enc", [P, D])
        coef = [sb(f"coef{a}", [P, NE, NC * n]) for a, n in enumerate((R0, R1))]
        mask = [sb(f"mask{a}", [P, NE, NC * n], u8) for a, n in enumerate((R0, R1))]
        wsum = sb("wsum", [P, NC, P])
        w_h, w_l = (select[:, k * NB:(k + 1) * NB, :].rearrange("p b c -> p (b c)").rearrange("p (k n) -> p k n", k=NC)
                    for k in range(2))
        wb_h = sb("wb_h", [P, NC, D], f32r)
        wb_l = sb("wb_l", [P, NC, D], f32r)
        a1_nat = sb("a1_nat", [P, D])
        b1_t = sb("b1_t", [P, E1 * NC, R])
        b0_t = sb("b0_t", [P, E0 * NC, R])
        b0_h = sb("b0_h", [P, NC, 2, K0], f32r)
        b0_l = sb("b0_l", [P, NC, 2, K0], f32r)
        b1_h = sb("b1_h", [P, NC, K1], f32r)
        b1_l = sb("b1_l", [P, NC, K1], f32r)
        mxh = sb("mxh", [P, NC, NX], f32r)
        mxl = sb("mxl", [P, NC, NX], f32r)
        enc_up, enc_low, g_parts = (mxl[:, k, 0:D] for k in range(3))
        bmh = sb("bmh", [P, NX], f32r)
        bml = sb("bml", [P, NX], f32r)
        m2h = sb("m2h", [P, D], f32r)
        m2l = sb("m2l", [P, D], f32r)
        bias_b = sb("bias_b", [P, D])

        xn = sb("xn", [P, 3, 2, T])
        xg = [sb(f"xg{k}", [P, 2, T], f32r) for k in range(3)]
        wg_up = [sb(f"wg_up{k}", [P, 2, QB // 2, H], f32r) for k in range(3)]
        wg_low = [sb(f"wg_low{k}", [P, QB // 2, H], f32r) for k in range(3)]
        hact = sb("hact", [P, 3, 2, T])
        ysum = sb("ysum", [P, 3, NC, QB, C])
        y0 = sb("y0", [P, 3, NC, QB, C])
        mid = sb("mid", [P, NT, NM])

        r0 = [sb(f"r0_{k}", [P, NT, E0]) for k in range(7)]
        s0 = [sb(f"s0_{k}", [P, NT]) for k in range(8)]
        gates0 = sb("gates0", [P, NT, E0])
        lang = sb("lang", [P, NT, E1])

        xs = dft_sb
        xth, xtl = ([buf[:, part, :].rearrange("p (k n) -> p k n", k=NC) for buf in xg] for part in range(2))
        gm = sb("gm", [P, 3, 2, K0])
        gmt = [buf[:, :, :].rearrange("p b h -> p (b h)") for buf in wg_low]
        gh = sb("gh", [P, 3, K1])
        ght_h, ght_l = ([buf[:, part, :, :].rearrange("p b h -> p (b h)") for buf in wg_up] for part in range(2))
        r1 = [sb(f"r1_{k}", [P, E1]) for k in range(7)]
        s1 = [sb(f"s1_{k}", [P, 1]) for k in range(9)]
        o_sb = wbase_nat

        ids_in, lens_in, sess_in, bsess_in, w2_in, b2_in = map(sem, ("ids_in", "lens_in", "sess_in", "bsess_in", "w2_in", "b2_in"))
        routers_in, coef_in, dft_in, enc_in = map(sem, ("routers_in", "coef_in", "dft_in", "enc_in"))
        w_in, a1_in, b1_in, b0_in, bias_in = map(sem, ("w_in", "a1_in", "b1_in", "b0_in", "bias_in"))
        wbase_in = [sem(f"wbase_in{k}") for k in range(2)]
        table_used = sem("table_used")
        zeroed, consts, ident_ready = sem("zeroed"), sem("consts"), sem("ident_ready")
        prep, bias_hot = sem("prep"), sem("bias_hot")
        select_first, select_last = sem("select_first"), sem("select_last")
        id_sel_ready = sem("id_sel_ready")
        first_doubled, rest_doubled, pair_ready = sem("first_doubled"), sem("rest_doubled"), sem("pair_ready")
        wsel_done, small_done = sem("wsel_done"), sem("small_done")
        wsess_split, wsel_saved, hbias_saved = sem("wsess_split"), sem("wsel_saved"), sem("hbias_saved")
        routersT_saved, wsum_step = sem("routersT_saved"), sem("wsum_step")
        w_h_ready, w_split, b1_split = sem("w_h_ready"), sem("w_split"), sem("b1_split")
        b0_split = [sem(f"b0_split{k}") for k in range(2)]
        wbh_saved = sem("wbh_saved")
        x1_in = [sem(f"x1_in{k}") for k in range(3)]
        xh_ready, xl_ready, wb_ready = sem("xh_ready"), sem("xl_ready"), sem("wb_ready")
        a_done, h_ready = sem("a_done"), sem("h_ready")
        y_done, ysum_ready, y0_ready = sem("y_done"), sem("ysum_ready"), sem("y0_ready")
        mid_done, mid_saved = sem("mid_done"), sem("mid_saved")
        g_done, g_up_saved, g_low_saved, wb_done, wb_saved = map(sem, ("g_done", "g_up_saved", "g_low_saved", "wb_done", "wb_saved"))
        enc_up_ready, enc_low_ready = sem("enc_up_ready"), sem("enc_low_ready")
        a1t_done, a1h_ready, a1l_ready, wr1_split = sem("a1t_done"), sem("a1h_ready"), sem("a1l_ready"), sem("wr1_split")
        m1_done, mx_ready, mxh_ready, mxl_ready = sem("m1_done"), sem("mx_ready"), sem("mxh_ready"), sem("mxl_ready")
        m2_done, m2h_ready, m2l_ready = sem("m2_done"), sem("m2h_ready"), sem("m2l_ready")
        bm_done, bmh_ready, bml_ready = sem("bm_done"), sem("bmh_ready"), sem("bml_ready")
        route0, gap0_ready, exp0_ready, gates0_ready = sem("route0"), sem("gap0_ready"), sem("exp0_ready"), sem("gates0_ready")
        x2_in = [sem(f"x2_in{k}") for k in range(3)]
        xt_done, xth_ready, xtl_ready = sem("xt_done"), sem("xth_ready"), sem("xtl_ready")
        gm_ready, gmt_done, gmth_ready, gmtl_ready = sem("gm_ready"), sem("gmt_done"), sem("gmth_ready"), sem("gmtl_ready")
        l1_done, x_done, route1, gap1_ready, exp1_ready = sem("l1_done"), sem("x_done"), sem("route1"), sem("gap1_ready"), sem("exp1_ready")
        gh_ready, ght_done, ghth_ready, ghtl_ready = sem("gh_ready"), sem("ght_done"), sem("ghth_ready"), sem("ghtl_ready")
        out_done, out_saved, half_saved = sem("out_done"), sem("out_saved"), sem("half_saved")
        stored = [sem(f"stored{k}") for k in range(3)]

        bank_a, bank_y, bank_mid = bank[0:2], (bank[2], bank[3], bank[5]), bank[4]
        slots = [(bank[0], bank[1]), (bank[2], bank[3]), (bank[4], bank[5])]
        bank_g, bank_x = bank[6], bank[7]
        bank_bm = bank[5], bank[3]
        bank_wb = bank[4:8]
        bank_small, bank_g_t, bank_a1 = bank[2], bank[3], bank[5]
        psum_hbias = bank_small[:, 0:NB]
        psum_routers = bank_small[:, NB:NB + NC * (NM + E1)].rearrange("p (k n) -> p k n", k=NC)

        def select_part(engine, k):
            n = NB // 2
            return engine.tensor_tensor(
                select[:, k * n:(k + 1) * n, :],
                id_sel[:, :, :].rearrange("p j b -> p (j b)")[:, k * n:(k + 1) * n].unsqueeze(2).to_broadcast([P, n, C]),
                delta[:, :].unsqueeze(1).to_broadcast([P, n, C]), ALU.mult)

        block = ctx.enter_context(nc.Block())

        @block.sync
        def _(sp):
            def load(t):
                if not t.real:
                    return
                if t.after(3):
                    sp.wait_ge(xl_ready, t.count(2, -4))
                for half in range(2):
                    sp.dma_start(xn[half * HP:(half + 1) * HP, t.slot, :, :],
                                 x_groups[:, ds(t.count(), 1), :, :].squeeze(1)).then_inc(x1_in[t.slot], 16)

            def double_w(first, last, doubled):
                for j in range(2):
                    here, there = slice(j * HP, (j + 1) * HP), slice((1 - j) * HP, (2 - j) * HP)
                    sp.dma_start(w_up[there, j, first:last, :], w_up[here, j, first:last, :]).then_inc(doubled, 16)

            sp.dma_start(id_b[:, :], session_ids.partition_broadcast(P)).then_inc(ids_in, 16)
            sp.dma_start(cc_b[:, :], channel_counts.partition_broadcast(P)).then_inc(ids_in, 16)
            sp.dma_start(w_sess[:, :, :], W_sess.rearrange("(j s) c h -> (s c) j h", j=2)).then_inc(sess_in, 16)
            for k in range(2):
                sp.dma_start(wbase_nat[:, k * NC // 2:(k + 1) * NC // 2, :],
                             W_base.rearrange("(k p) n -> p k n", p=P)[:, k * NC // 2:(k + 1) * NC // 2, :]).then_inc(wbase_in[k], 16)
            sp.dma_start(b_sess2[:, :, :], b_sess.unsqueeze(1).to_broadcast([S, 2, H])).then_inc(bsess_in, 16)
            sp.dma_start(routers[0:K0, :], A0.rearrange("e r t -> (e r) t")).then_inc(routers_in, 16)
            sp.dma_start(routers[K0:NM, :], Wr0).then_inc(routers_in, 16)
            sp.dma_start(routers[NM:NM + E1, :], Wr1).then_inc(routers_in, 16)
            sp.dma_start(dft_sb[:, :, :], dft.rearrange("(p k) n -> p k n", p=P)).then_inc(dft_in, 16)
            load(Tile(None, 0, 3, NT))
            sp.wait_ge(wsel_saved, 3)
            double_w(0, 4, first_doubled)
            load(Tile(None, 1, 3, NT))
            load(Tile(None, 2, 3, NT))
            sp.wait_ge(wsel_saved, 12)
            double_w(4, NT, rest_doubled)
            load(Tile(None, 3, 3, NT))
            load(Tile(None, 4, 3, NT))
            sp.dma_start(a1_nat[:, :], A1.rearrange("e r d -> (e r) d")).then_inc(a1_in, 16)
            for k in range(2):
                sp.dma_start(w_nat[:, k * NC // 2:(k + 1) * NC // 2, :],
                             W.rearrange("(k p) n -> p k n", p=P)[:, k * NC // 2:(k + 1) * NC // 2, :]).then_inc(w_in, 16)
                load(Tile(None, 5 + k, 3, NT))
            sp.dma_start(b1_t[:, :, :], B1.rearrange("e (k p) r -> p (e k) r", p=P)).then_inc(b1_in, 16)
            load(Tile(None, 7, 3, NT))
            sp.dma_start(b0_t[:, :, :], B0.rearrange("e (k p) r -> p (e k) r", p=P)).then_inc(b0_in, 16)
            sp.dma_start(bias_b[:, :], b_base.partition_broadcast(P)).then_inc(bias_in, 16)
            run_tiles(sp, 3, NT, 8, NT - 1, load, head=8)

            sp.wait_ge(g_done, 1)

            def load2(t):
                if not t.real:
                    return
                if t.after(3):
                    sp.wait_ge(xt_done, t.count(1, -2))
                sp.dma_start(xs[:, t.slot, :], x_tiles[:, ds(t.count(), 1), :].squeeze(1)).then_inc(x2_in[t.slot], 16)

            def store(t):
                if not t.real:
                    return
                sp.wait_ge(half_saved, t.count(1, 1))
                if t.n is None and t.c == NT - 1:
                    sp.dma_start(out_tiles[:, t.c, 0:OA], o_sb[:, t.slot, 0:OA]).then_inc(stored[t.slot], 16)
                    sp.wait_ge(out_saved, NT)
                    sp.dma_start(out_tiles[:, t.c, OA:D], o_sb[:, t.slot, OA:D]).then_inc(stored[t.slot], 16)
                    return
                sp.wait_ge(out_saved, t.count(1, 1))
                sp.dma_start(out_tiles[:, ds(t.count(), 1), :].squeeze(1), o_sb[:, t.slot, :]).then_inc(stored[t.slot], 16)

            def step(t):
                load2(t + 2)
                store(t - 2)

            run_tiles(sp, 3, NT, -2, NT + 1, step)
            for k in range(3):
                sp.wait_ge(stored[k], 16 * (len(range(k, NT, 3)) + (k == (NT - 1) % 3)))

        @block.gpsimd
        def _(pool):
            g = nc.gpsimd
            g.memset(ident[:, :], 0.0).then_inc(zeroed, 1)
            g.memset(delta[:, :], 0.0).then_inc(zeroed, 1)
            g.memset(quad[:, :], 1.0).then_inc(zeroed, 1)
            g.iota(p_col[:, :], pattern=[[0, 1]], base=0, channel_multiplier=1,
                   allow_small_or_imprecise_dtypes=True).then_inc(consts, 1)
            g.iota(t_col[:, :], pattern=[[P, NC]], base=0, channel_multiplier=1,
                   allow_small_or_imprecise_dtypes=True).then_inc(consts, 1)
            g.iota(rev0[:, :], pattern=[[-1, E0]], base=E0, channel_multiplier=0,
                   allow_small_or_imprecise_dtypes=True).then_inc(consts, 1)
            g.iota(rev1[:, :], pattern=[[-1, E1]], base=E1, channel_multiplier=0,
                   allow_small_or_imprecise_dtypes=True).then_inc(consts, 1)
            g.iota(lane1[:, :], pattern=[[1, E1]], base=0, channel_multiplier=0,
                   allow_small_or_imprecise_dtypes=True).then_inc(consts, 1)
            pool.wait_ge(zeroed, 3)
            for q in range(QB):
                g.affine_select(out=delta[:, :], in_=delta[:, :], compare_op=ALU.not_equal, fill=1.0,
                                base=-C * q, pattern=[[-1, C]], channel_multiplier=1).then_inc(zeroed, 1)
                pool.wait_ge(zeroed, 4 + q)
            g.affine_select(out=quad[:, :], in_=quad[:, :], compare_op=ALU.is_ge, fill=0.0,
                            base=0, pattern=[[-C, QB]], channel_multiplier=1).then_inc(zeroed, 1)
            pool.wait_ge(zeroed, 4 + QB)
            g.affine_select(out=quad[:, :], in_=quad[:, :], compare_op=ALU.is_ge, fill=0.0,
                            base=C - 1, pattern=[[C, QB]], channel_multiplier=-1).then_inc(zeroed, 1)
            g.affine_select(out=ident[:, :], in_=ident[:, :], compare_op=ALU.not_equal, fill=1.0,
                            base=0, pattern=[[-1, P]], channel_multiplier=1).then_inc(ident_ready, 1)
            g.memset(w2_blk[:, :], 0.0).then_inc(zeroed, 1)
            g.memset(enc[:, :], 0.0).then_inc(zeroed, 1)
            g.memset(wsum[:, :, :], 0.0).then_inc(zeroed, 1)
            pool.wait_ge(id_sel_ready, 2)
            select_part(g, 3).then_inc(select_last, 1)
            pool.wait_ge(zeroed, 8 + QB)
            for half in range(2):
                g.dma_start(enc[half * HP:half * HP + R0, :], enc0).then_inc(enc_in, 16)
                g.dma_start(enc[half * HP + R0:half * HP + RE, :], enc1).then_inc(enc_in, 16)
            g.dma_start(w2_blk[0:H, 0:C], W2).then_inc(w2_in, 16)
            g.dma_start(w2_blk[H:2 * H, C:2 * C], W2).then_inc(w2_in, 16)
            g.dma_start(sl_b[:, :], seq_lens.partition_broadcast(P)).then_inc(lens_in, 16)
            g.dma_start(b2_b[:, :], b2.partition_broadcast(P)).then_inc(b2_in, 16)

            def spread_w(t):
                if not t.real:
                    return
                if t.after(3):
                    pool.wait_ge(a_done, t.count(2, -4))
                if t.n is None and t.c == 0:
                    pool.wait_ge(pair_ready, 1)
                    pool.wait_ge(wsel_saved, 3)
                    pool.wait_ge(first_doubled, 32)
                if t.n is None and t.c == 4:
                    pool.wait_ge(wsel_saved, 12)
                    pool.wait_ge(rest_doubled, 32)
                up = [P, 2, QB // 2, H]
                g.tensor_tensor(wg_up[t.slot][:, :, :, :], w_up[:, :, ds(t.count(), 1), :].to_broadcast(up),
                                pair[:, :].unsqueeze(1).unsqueeze(3).to_broadcast(up), ALU.mult).then_inc(wb_ready, 1)
                low = [P, QB // 2, H]
                g.tensor_tensor(wg_low[t.slot][:, :, :], w_low[:, ds(t.count(), 1), :].to_broadcast(low),
                                pair[:, :].unsqueeze(2).to_broadcast(low), ALU.mult).then_inc(wb_ready, 1)

            def mask_y(t):
                if not t.real:
                    return
                pool.wait_ge(ysum_ready, t.count(1, 1))
                if t.after(3):
                    pool.wait_ge(mid_done, t.count(1, -2))
                g.tensor_tensor(y0[:, t.slot, :, :, :], ysum[:, t.slot, :, :, :],
                                t_mask[:, :, ds(t.count(QB), QB)].unsqueeze(3).to_broadcast([P, NC, QB, C]),
                                ALU.mult).then_inc(y0_ready, 1)

            def step(t):
                spread_w(t + 1)
                mask_y(t - 1)

            run_tiles(pool, 3, NT, -1, NT + 1, step)

            def gate_l0(t):
                if not t.real:
                    return
                if t.after(3):
                    pool.wait_ge(gmt_done, t.count(1, -2))
                shape = [P, 2, E0, R]
                g.tensor_tensor(gm[:, t.slot, :, :].rearrange("p a (e r) -> p a e r", e=E0),
                                mid[:, ds(t.count(), 1), 0:K0].rearrange("p a (e r) -> p a e r", e=E0).to_broadcast(shape),
                                gates0[:, ds(t.count(), 1), :].unsqueeze(3).to_broadcast(shape),
                                ALU.mult).then_inc(gm_ready, 1)

            pool.wait_ge(gates0_ready, 1)
            run_tiles(pool, 3, NT, -2, NT + 1, lambda t: gate_l0(t + 2))

        @block.scalar
        def _(act):
            a = nc.scalar
            act.wait_ge(consts, 5)
            a.activation(table[:, 0:1], p_col[:, :], ACT.Gelu).then_inc(table_used, 1)

            act.wait_ge(ids_in, 32)
            for dst, src in ((coef, (coefs0, coefs1)), (mask, (mask0, mask1))):
                act.dma_start(dst[0][:, :, :], src[0].rearrange("e (p k) r -> p e (k r)", p=P)).then_inc(coef_in, 16)
                act.dma_start(dst[1][:, :, :], src[1].rearrange("e (p k) r -> p e (k r)", p=P)).then_inc(coef_in, 16)

            def split_x(t):
                act.wait_ge(x1_in[t.slot], t.round(32, 32))
                a.activation(xg[t.slot][:, :, :], xn[:, t.slot, :, :], ACT.Copy).then_inc(xh_ready, 1)

            def gelu(t):
                if (t + 2).real and not t.real:
                    split_x(t + 2)
                if not t.real:
                    return
                for j in range(2):
                    act.wait_ge(a_done, t.count(2, j + 1))
                    if t.after(3) and j == 0:
                        act.wait_ge(y_done, t.count(1, -2))
                    a.activation(hact[:, t.slot, j, :], bank_a[j][:, :], ACT.Gelu,
                                 bias=h_bias[:, ds(t.count(2, j), 1)]).then_inc(h_ready, 1)
                if (t + 2).real:
                    split_x(t + 2)

            def save_wsel(k):
                act.wait_ge(wsel_done, k + 1)
                four = slice(k * 4, (k + 1) * 4)
                gathered = bank[k][:, :].rearrange("p (g a h) -> p g a h", g=4, a=2)
                for j in range(2):
                    half = slice(j * HP, (j + 1) * HP)
                    a.activation(w_up[half, j, four, :], gathered[half, :, 0, :], ACT.Copy).then_inc(wsel_saved, 1)
                a.activation(w_low[:, four, :], gathered[:, :, 1, :], ACT.Copy).then_inc(wsel_saved, 1)

            save_wsel(0)
            save_wsel(1)
            save_wsel(2)
            save_wsel(3)
            act.wait_ge(enc_in, 64)
            a.activation(enc_up, enc[:, :], ACT.Copy).then_inc(enc_up_ready, 1)
            split_x(Tile(None, 0, 3, NT))
            split_x(Tile(None, 1, 3, NT))
            act.wait_ge(g_done, 1)
            a.activation(g_parts, bank_g_t[:, :], ACT.Copy).then_inc(g_up_saved, 1)
            act.wait_ge(small_done, 1)
            for k in range(2):
                a.activation(h_bias[k * H:(k + 1) * H, :], psum_hbias[k * H:(k + 1) * H, k:NB:2],
                             ACT.Copy).then_inc(hbias_saved, 1)
            act.wait_ge(hbias_saved, 2)
            gelu(Tile(None, 0, 3, NT))

            def wb_up(m):
                act.wait_ge(wb_done, m + 1)
                a.activation(wb_h[:, m, :], bank_wb[m][:, :], ACT.Copy).then_inc(wbh_saved, 1)

            wb_up(0)
            wb_up(1)
            gelu(Tile(None, 1, 3, NT))
            wb_up(2)
            wb_up(3)

            def gelu_and_w(t):
                gelu(t)
                if t.n is None and t.c >= NT - 2:
                    act.wait_ge(w_in, 32)
                    for k in range(2 * (t.c - NT + 2), 2 * (t.c - NT + 3)):
                        a.activation(w_h[:, k, :], w_nat[:, k, :], ACT.Copy).then_inc(w_h_ready, 1)

            run_tiles(act, 3, NT, 2, NT - 1, gelu_and_w)

            a.activation(table[:, 1:2], p_col[:, :], ACT.Sigmoid).then_inc(table_used, 1)

            act.wait_ge(a1t_done, 1)
            a.activation(mxh[:, :, 0:K1], bank_a1[:, :].rearrange("p (k n) -> p k n", k=NC), ACT.Copy).then_inc(a1h_ready, 1)
            act.wait_ge(gap0_ready, 1)
            a.activation(s0[5][:, :], s0[4][:, :], ACT.Sigmoid, scale=-1.0).then_inc(exp0_ready, 1)
            a.activation(s0[6][:, :], s0[4][:, :], ACT.Sigmoid).then_inc(exp0_ready, 1)
            for d in range(NC):
                act.wait_ge(mx_ready, d + 1)
                a.activation(mxh[:, d, L1C:NX], bank[d][:, :], ACT.Copy).then_inc(mxh_ready, 1)
            act.wait_ge(m2_done, 1)
            a.activation(m2h[:, :], bank[4][:, :], ACT.Copy).then_inc(m2h_ready, 1)

            def step(t):
                u = t + 1
                if u.real:
                    act.wait_ge(xt_done, u.count(1, 1))
                    if u.after(3):
                        act.wait_ge(x_done, u.count(1, -2))
                    a.activation(xth[u.slot][:, :, :], bank_x[:, :].rearrange("p (k n) -> p k n", k=NC),
                                 ACT.Copy).then_inc(xth_ready, 1)
                u = t + 1
                if u.real:
                    act.wait_ge(gmt_done, u.count(1, 1))
                    a.activation(gmt[u.slot][:, :], bank_g[:, P:2 * P], ACT.Copy).then_inc(gmth_ready, 1)
                u = t - 1
                if u.real:
                    act.wait_ge(gap1_ready, u.count(1, 1))
                    a.activation(s1[5][:, :], s1[2][:, :], ACT.Sigmoid, scale=-1.0).then_inc(exp1_ready, 1)
                    a.activation(s1[6][:, :], s1[2][:, :], ACT.Sigmoid).then_inc(exp1_ready, 1)
                if u.real:
                    act.wait_ge(ght_done, u.count(1, 1))
                    if u.after(3):
                        act.wait_ge(out_done, u.count(2, -4))
                    a.activation(ght_h[u.slot][:, :], bank_g[:, 0:P], ACT.Copy).then_inc(ghth_ready, 1)

            step(Tile(None, -1, 3, NT))
            for k in range(2):
                act.wait_ge(bm_done, k + 1)
                a.activation(bmh[:, half_x[k]], bank_bm[k][:, 0:(NX0, NX1)[k]], ACT.Copy).then_inc(bmh_ready, 1)
            run_tiles(act, 3, NT, 0, NT + 1, step)

        @block.vector
        def _(dve):
            v = nc.vector
            dve.wait_ge(consts, 5)
            v.tensor_scalar(quad_tmp[:, 0:1], p_col[:, :], float(C), None, ALU.is_ge).then_inc(prep, 1)
            dve.wait_ge(prep, 1)
            for q in range(2, QB):
                src, dst = (quad_tmp[:, q % 2:q % 2 + 1], quad_tmp[:, (q + 1) % 2:(q + 1) % 2 + 1])
                if q == QB - 1:
                    dst = quad_no[:, :]
                v.scalar_tensor_tensor(dst, p_col[:, :], float(C * q), src, ALU.is_ge, ALU.add).then_inc(prep, 1)
                dve.wait_ge(prep, q)
            v.scalar_tensor_tensor(in_quad[:, :], quad_no[:, :], -float(C), p_col[:, :], ALU.mult, ALU.add).then_inc(prep, 1)
            dve.wait_ge(ids_in, 32)
            for j in range(2):
                v.tensor_scalar(id_eq[:, j, :], id_b[:, :], -float(j * S // 2), quad_no[:, :], ALU.add,
                                ALU.is_equal).then_inc(prep, 1)
            dve.wait_ge(prep, QB + 2)
            for j in range(2):
                v.scalar_tensor_tensor(id_sel[:, j, :], cc_b[:, :], in_quad[:, :], id_eq[:, j, :], ALU.is_gt,
                                       ALU.mult).then_inc(id_sel_ready, 1)
            dve.wait_ge(id_sel_ready, 2)
            dve.wait_ge(zeroed, 5 + QB)
            select_part(v, 0).then_inc(select_first, 1)
            v.tensor_tensor(pair[:, :], quad[:, 0:QB // 2], quad[:, QB // 2:QB], ALU.add).then_inc(pair_ready, 1)
            dve.wait_ge(sess_in, 16)
            v.tensor_copy(w_sess2[:, :, 0, :], w_sess[:, :, :]).then_inc(wsess_split, 1)
            select_part(v, 2).then_inc(select_first, 1)
            dve.wait_ge(wsess_split, 1)
            v.tensor_tensor(w_sess2[:, :, 1, :], w_sess[:, :, :], w_sess2[:, :, 0, :].bitcast(fp32),
                            ALU.subtract).then_inc(wsess_split, 1)
            select_part(v, 1).then_inc(select_last, 1)
            v.tensor_scalar(one_hot[:, :], id_b[0:S, :], p_col[0:S, :], None, ALU.is_equal).then_inc(bias_hot, 1)

            def step(t):
                u = t + 1
                if u.real:
                    dve.wait_ge(xh_ready, u.count(1, 1))
                    for j in range(2):
                        low = slice((1 - j) * HP, (2 - j) * HP)
                        v.tensor_tensor(xg[u.slot][low, j, :], xn[low, u.slot, j, :], xg[u.slot][low, j, :].bitcast(fp32),
                                        ALU.subtract).then_inc(xl_ready, 1)
                u = t - 1
                if u.real:
                    dve.wait_ge(y_done, u.count(1, 1))
                    if u.after(3):
                        dve.wait_ge(y0_ready, u.count(1, -2))
                    v.tensor_tensor(ysum[:, u.slot, :, :, :].rearrange("p k b c -> p (k b) c"),
                                    bank_y[u.slot][:, :].rearrange("p (n c) -> p n c", c=C),
                                    b2_b[:, :].unsqueeze(1).to_broadcast([P, NC * QB, C]), ALU.add).then_inc(ysum_ready, 1)
                u = t - 2
                if u.real:
                    dve.wait_ge(mid_done, u.count(1, 1))
                    v.tensor_copy(mid[:, ds(u.count(), 1), :].squeeze(1), bank_mid[:, 0:NM]).then_inc(mid_saved, 1)

            dve.wait_ge(coef_in, 64)
            for a in range(2):
                v.tensor_tensor(coef[a][:, :, :], coef[a][:, :, :], mask[a][:, :, :], ALU.mult).then_inc(wsum_step, 1)
            dve.wait_ge(wsum_step, 2)
            dve.wait_ge(zeroed, 8 + QB)
            parts = [(wsum[:, :, cols], [coef[a][:, e, :].rearrange("p (k r) -> p k r", k=NC) for e in range(NE)])
                     for a, cols in enumerate((slice(0, R0), slice(R0, RE)))]
            for dst, terms in parts:
                v.tensor_tensor(dst, terms[0], terms[1], ALU.add).then_inc(wsum_step, 1)
            for e in range(2, NE):
                dve.wait_ge(wsum_step, 2 * e)
                for dst, terms in parts:
                    v.tensor_tensor(dst, dst, terms[e], ALU.add).then_inc(wsum_step, 1)
            dve.wait_ge(wsum_step, 2 * NE)
            v.tensor_copy(wsum[:, :, HP:HP + RE], wsum[:, :, 0:RE]).then_inc(wsum_step, 1)
            dve.wait_ge(enc_up_ready, 1)
            v.tensor_tensor(enc_low[0:HP, :], enc[0:HP, :], enc_up[0:HP, :].bitcast(fp32), ALU.subtract).then_inc(enc_low_ready, 1)
            step(Tile(None, -1, 3, NT))
            dve.wait_ge(lens_in, 16)
            for k in range(NC):
                v.tensor_scalar(t_mask[:, k, :], sl_b[:, :], t_col[:, k:k + 1], None, ALU.is_gt).then_inc(prep, 1)
            dve.wait_ge(b2_in, 16)
            dve.wait_ge(g_up_saved, 1)
            v.tensor_tensor(g_parts[HP:P, :], bank_g_t[HP:P, :], g_parts[HP:P, :].bitcast(fp32), ALU.subtract).then_inc(g_low_saved, 1)
            step(Tile(None, 0, 3, NT))
            dve.wait_ge(hbias_saved, 2)
            v.tensor_copy(routersT[:, :, :], psum_routers).then_inc(routersT_saved, 1)
            step(Tile(None, 1, 3, NT))

            def wb_low(m):
                dve.wait_ge(wbh_saved, m + 1)
                v.tensor_tensor(wb_l[:, m, :], bank_wb[m][:, :], wb_h[:, m, :].bitcast(fp32), ALU.subtract).then_inc(wb_saved, 1)

            wb_low(0)
            wb_low(1)

            def split_scaled(parts, src, scale, s):
                src = src[:, :, :].rearrange("p (e k) r -> p k e r", k=NC)
                high, low = (part.rearrange("p k (e r) -> p k e r", r=R) for part in parts)
                v.tensor_scalar(high, src, scale, None, ALU.mult).then_inc(s, 1)
                dve.wait_ge(s, 1)
                for k in range(NC):
                    v.scalar_tensor_tensor(low[:, k], src[:, k], scale, high[:, k].bitcast(fp32), ALU.mult,
                                           ALU.subtract).then_inc(s, 1)

            def step_and_weights(t):
                step(t)
                if t.n is None and 2 <= t.c < NC:
                    wb_low(t.c)
                if t.n is None and t.c in (NT - 2, NT - 1):
                    for k in range(2 * (t.c - NT + 2), 2 * (t.c - NT + 3)):
                        dve.wait_ge(w_h_ready, k + 1)
                        v.tensor_tensor(w_l[:, k, :], w_nat[:, k, :], w_h[:, k, :].bitcast(fp32), ALU.subtract).then_inc(w_split, 1)
                if t.n is None and t.c == NT:
                    dve.wait_ge(b1_in, 16)
                    split_scaled((b1_h[:, :, :], b1_l[:, :, :]), b1_t, SCALE1, b1_split)

            run_tiles(dve, 3, NT, 2, NT + 1, step_and_weights)

            done = [0]

            def then(ins, s):
                done[0] += 1
                ins.then_inc(s, 1)
                dve.wait_ge(s, done[0])

            dve.wait_ge(mid_saved, NT)
            logits = mid[:, :, K0:NM]
            wide = [P, NT, E0]
            rev = rev0[:, :].unsqueeze(1).to_broadcast(wide)

            def over(s):
                return s[:, :].unsqueeze(2).to_broadcast(wide)

            def first_max(values, top, eq, ranked, best, hot):
                then(v.tensor_reduce(top[:, :], values, X, ALU.max), route0)
                then(v.tensor_tensor(eq[:, :, :], values, over(top), ALU.is_equal), route0)
                then(v.tensor_tensor(ranked[:, :, :], eq[:, :, :], rev, ALU.mult), route0)
                then(v.tensor_reduce(best[:, :], ranked[:, :, :], X, ALU.max), route0)
                then(v.tensor_tensor(hot[:, :, :], ranked[:, :, :], over(best), ALU.is_equal), route0)

            first_max(logits, s0[0], r0[0], r0[1], s0[1], r0[2])
            then(v.scalar_tensor_tensor(r0[3][:, :, :], r0[2][:, :, :], NEG, logits, ALU.mult, ALU.add), route0)
            first_max(r0[3][:, :, :], s0[2], r0[0], r0[1], s0[3], r0[4])
            v.tensor_tensor(s0[4][:, :], s0[2][:, :], s0[0][:, :], ALU.subtract).then_inc(gap0_ready, 1)
            dve.wait_ge(exp0_ready, 2)
            then(v.tensor_tensor(r0[5][:, :, :], r0[2][:, :, :], over(s0[5]), ALU.mult), route0)
            then(v.tensor_tensor(r0[6][:, :, :], r0[4][:, :, :], over(s0[6]), ALU.mult), route0)
            v.tensor_tensor(gates0[:, :, :], r0[5][:, :, :], r0[6][:, :, :], ALU.add).then_inc(gates0_ready, 1)

            dve.wait_ge(b0_in, 16)
            for k in range(2):
                split_scaled((b0_h[:, :, k, :], b0_l[:, :, k, :]), b0_t, SCALE0, b0_split[k])

            v.tensor_copy(mxh[:, :, K1:L1C], routersT[:, :, NM:NM + E1]).then_inc(wr1_split, 1)
            dve.wait_ge(wr1_split, 1)
            v.tensor_tensor(mxl[:, :, K1:L1C], routersT[:, :, NM:NM + E1], mxh[:, :, K1:L1C].bitcast(fp32),
                            ALU.subtract).then_inc(wr1_split, 1)
            dve.wait_ge(a1h_ready, 1)
            v.tensor_tensor(mxl[:, :, 0:K1], bank_a1[:, :].rearrange("p (k n) -> p k n", k=NC),
                            mxh[:, :, 0:K1].bitcast(fp32), ALU.subtract).then_inc(a1l_ready, 1)
            for d in range(NC + 1):
                if d < NC:
                    dve.wait_ge(m1_done, d + 1)
                    diag = bank[d][:, d * P:(d + 1) * P]
                    v.tensor_tensor(diag, diag, ident[:, :], ALU.add).then_inc(mx_ready, 1)
                if d >= 1:
                    dve.wait_ge(mxh_ready, d)
                    v.tensor_tensor(mxl[:, d - 1, L1C:NX], bank[d - 1][:, :], mxh[:, d - 1, L1C:NX].bitcast(fp32),
                                    ALU.subtract).then_inc(mxl_ready, 1)
            for q in range(QB):
                v.tensor_copy(id_tok[q * C:(q + 1) * C, :], id_b[q * C:(q + 1) * C, q:NB:QB]).then_inc(prep, 1)
            dve.wait_ge(prep, 2 * QB + 2 + NC)
            v.tensor_tensor(lang[:, :, :], id_tok[:, :].unsqueeze(2).to_broadcast([P, NT, E1]),
                            lane1[:, :].unsqueeze(1).to_broadcast([P, NT, E1]), ALU.is_equal).then_inc(prep, 1)
            dve.wait_ge(prep, 2 * QB + 3 + NC)
            v.tensor_scalar(lang[:, :, :], lang[:, :, :], LANG_BIAS, None, ALU.mult).then_inc(prep, 1)
            dve.wait_ge(m2h_ready, 1)
            v.tensor_tensor(m2l[:, :], bank[4][:, :], m2h[:, :].bitcast(fp32), ALU.subtract).then_inc(m2l_ready, 1)
            dve.wait_ge(bias_in, 16)

            ROUTE1 = 11

            l, w, hot1, l2, w2_, gate, hot2g = (r1[k][:, :] for k in range(7))
            top, best, gap, top2, best2, g1, g2 = (s1[k][:, :] for k in range(7))

            def chained(u, steps):
                if u.real:
                    dve.wait_ge(route1, u.count(ROUTE1, steps))

            def output(u, h):
                if u.real:
                    dve.wait_ge(out_done, u.count(2, h + 1))
                    if u.after(3) and h == 0:
                        dve.wait_ge(stored[u.slot], u.round(16))
                    cols, src = ((slice(0, OA), slots[u.slot][0][:, L1C:NX0]), (slice(OA, D), slots[u.slot][1][:, 0:NX1]))[h]
                    v.tensor_tensor(o_sb[:, u.slot, cols], src, bias_b[:, cols], ALU.add).then_inc((half_saved, out_saved)[h], 1)

            def step2(t):
                nxt, old = t + 1, t - 2
                if nxt.real:
                    dve.wait_ge(xth_ready, nxt.count(1, 1))
                    v.tensor_tensor(xtl[nxt.slot][:, :, :], bank_x[:, :].rearrange("p (k n) -> p k n", k=NC),
                                    xth[nxt.slot][:, :, :].bitcast(fp32), ALU.subtract).then_inc(xtl_ready, 1)
                u = t - 1
                chained(u, 6)
                if u.real:
                    v.tensor_reduce(top2, l2, X, ALU.max).then_inc(route1, 1)
                if nxt.real:
                    dve.wait_ge(gmth_ready, nxt.count(1, 1))
                    v.tensor_tensor(gmt[nxt.slot][K0:2 * K0, :], bank_g[K0:2 * K0, P:2 * P],
                                    gmt[nxt.slot][K0:2 * K0, :].bitcast(fp32), ALU.subtract).then_inc(gmtl_ready, 1)
                chained(u, 7)
                if u.real:
                    v.tensor_tensor(gap, top2, top, ALU.subtract).then_inc(gap1_ready, 1)
                    v.scalar_tensor_tensor(w2_, l2, top2, rev1[:, :], ALU.is_equal, ALU.mult).then_inc(route1, 1)
                if t.real and not t.last:
                    output(old, 0)
                chained(u, 8)
                if u.real:
                    v.tensor_reduce(best2, w2_, X, ALU.max).then_inc(route1, 1)
                if t.past:
                    output(u - 2, 0)
                chained(u, 9)
                if u.real:
                    dve.wait_ge(exp1_ready, u.count(2, 2))
                    v.tensor_scalar(hot2g, w2_, best2, g2, ALU.is_equal, ALU.mult).then_inc(route1, 1)
                if t.real and not t.last:
                    output(old, 1)
                chained(u, 10)
                if u.real:
                    v.scalar_tensor_tensor(gate, hot1, g1, hot2g, ALU.mult, ALU.add).then_inc(route1, 1)
                chained(u, 11)
                if u.real:
                    if u.after(3):
                        dve.wait_ge(ght_done, u.count(1, -2))
                    v.tensor_tensor(gh[:, u.slot, :].rearrange("p (e r) -> p e r", e=E1),
                                    slots[u.slot][0][:, 0:K1].rearrange("p (e r) -> p e r", e=E1),
                                    gate.unsqueeze(2).to_broadcast([P, E1, R]), ALU.mult).then_inc(gh_ready, 1)
                if t.past:
                    output(u - 2, 1)
                if not t.real:
                    output(old, 0)
                if not t.real and not t.past:
                    output(old, 1)
                if t.real:
                    dve.wait_ge(l1_done, t.count(1, 1))
                    v.tensor_tensor(l, slots[t.slot][0][:, K1:L1C], lang[:, ds(t.count(), 1), :].squeeze(1),
                                    ALU.add).then_inc(route1, 1)
                chained(t, 1)
                if t.real:
                    v.tensor_reduce(top, l, X, ALU.max).then_inc(route1, 1)
                chained(t, 2)
                if t.real:
                    v.scalar_tensor_tensor(w, l, top, rev1[:, :], ALU.is_equal, ALU.mult).then_inc(route1, 1)
                chained(t, 3)
                if t.real:
                    v.tensor_reduce(best, w, X, ALU.max).then_inc(route1, 1)
                chained(t, 4)
                if t.real:
                    v.tensor_scalar(hot1, w, best, None, ALU.is_equal).then_inc(route1, 1)
                chained(t, 5)
                if t.real:
                    v.scalar_tensor_tensor(l2, hot1, NEG, l, ALU.mult, ALU.add).then_inc(route1, 1)
                if u.real:
                    dve.wait_ge(ghth_ready, u.count(1, 1))
                    v.tensor_tensor(ght_l[u.slot][:, :], bank_g[:, 0:P], ght_h[u.slot][:, :].bitcast(fp32),
                                    ALU.subtract).then_inc(ghtl_ready, 1)
                if t.past:
                    output(old, 1)

            step2(Tile(None, -1, 3, NT))
            for k in range(2):
                dve.wait_ge(bmh_ready, k + 1)
                v.tensor_tensor(bml[:, half_x[k]], bank_bm[k][:, 0:(NX0, NX1)[k]],
                                bmh[:, half_x[k]].bitcast(fp32), ALU.subtract).then_inc(bml_ready, 1)
            run_tiles(dve, 3, NT, 0, NT + 1, step2)

        @block.tensor
        def _(pe):
            mm = nc.tensor.matmul
            def gather(first, last):
                for t in range(first, last):
                    for j in range(2):
                        done = mm(bank[t // 4][:, (t % 4) * 2 * H:(t % 4 + 1) * 2 * H],
                                  select[:, j * NB + t * QB:j * NB + (t + 1) * QB, :].rearrange("p b c -> p (b c)"),
                                  w_sess2[:, j, :, :].rearrange("p a h -> p (a h)"), start=(j == 0), stop=(j == 1))
                    if t % 4 == 3:
                        done.then_inc(wsel_done, 1)

            pe.wait_ge(ident_ready, 1)
            for _ in range(WARM_UP):
                mm(bank[7][:, 0:P], ident[:, :], ident[:, :], start=True, stop=True)
            def turn_wbase(k):
                if k % (NC // 2) == 0:
                    pe.wait_ge(wbase_in[k // (NC // 2)], 16)
                for m in range(NC):
                    mm(bank_wb[m][:, k * P:(k + 1) * P], wbase_nat[:, k, m * P:(m + 1) * P], ident[:, :],
                       start=(k == 0), stop=False)

            for k in range(NC // 2):
                turn_wbase(k)
            pe.wait_ge(wsess_split, 2)
            pe.wait_ge(select_first, 2)
            gather(0, NT // 2)
            pe.wait_ge(select_last, 2)
            gather(NT // 2, NT)
            for k in range(NC // 2, NC - 1):
                turn_wbase(k)
            pe.wait_ge(bsess_in, 16)
            pe.wait_ge(bias_hot, 1)
            pe.wait_ge(wsel_saved, 9)
            mm(psum_hbias, b_sess2[:, :, :].rearrange("s a h -> s (a h)"), one_hot[:, :], start=True, stop=True)
            pe.wait_ge(dft_in, 16)
            pe.wait_ge(wsum_step, 2 * NE + 1)
            pe.wait_ge(wsel_saved, 12)
            for k in range(NC):
                last = mm(bank_g_t[:, :], wsum[:, k, :], dft_sb[:, k, :], start=(k == 0), stop=(k == NC - 1))
            last.then_inc(g_done, 1)
            pe.wait_ge(routers_in, 48)
            n = NM + E1
            for k in range(NC):
                last = nc.tensor.transpose(psum_routers[:, k, :], routers[:, k * P:(k + 1) * P], ident[0:n, 0:n])
            last.then_inc(small_done, 1)
            turn_wbase(NC - 1)

            def step(t):
                u = t
                if u.real:
                    pe.wait_ge(xl_ready, u.count(2, 2))
                    pe.wait_ge(wb_ready, u.count(2, 2))
                    for j in range(2):
                        up = slice(j * HP, (j + 1) * HP)
                        if u.after(1):
                            pe.wait_ge(h_ready, u.count(2, j - 1))
                        else:
                            pe.wait_ge(wsel_saved, 3 * j + 3)
                        mm(bank_a[j][:, :], wg_up[u.slot][:, j, :, :].rearrange("p b h -> p (b h)"), xg[u.slot][:, j, :],
                           start=True, stop=False)
                        mm(bank_a[j][:, :], wg_low[u.slot][up, :, :].rearrange("p b h -> p (b h)"), xg[u.slot][up, j, :],
                           start=False, stop=True).then_inc(a_done, 1)
                u = t - 1
                if u.real:
                    if u.after(3):
                        pe.wait_ge(ysum_ready, u.count(1, -2))
                    elif u.c == 0:
                        pe.wait_ge(w2_in, 32)
                        pe.wait_ge(routersT_saved, 1)
                    else:
                        pe.wait_ge(*((g_low_saved, 1), (wb_saved, 2))[u.c - 1])
                    for j in range(2):
                        pe.wait_ge(h_ready, u.count(2, j + 1))
                        for k in range(NC):
                            last = mm(bank_y[u.slot][:, k * P + j * 2 * C:k * P + (j + 1) * 2 * C],
                                      hact[:, u.slot, j, k * P:(k + 1) * P], w2_blk[:, :], start=True, stop=True)
                    last.then_inc(y_done, 1)
                u = t - 2
                if u.real:
                    pe.wait_ge(y0_ready, u.count(1, 1))
                    if u.after(1):
                        pe.wait_ge(mid_saved, u.count())
                    if u.n is None and u.c == 0:
                        pe.wait_ge(wb_saved, 1)
                    for k in range(NC):
                        last = mm(bank_mid[:, 0:NM], y0[:, u.slot, k, :, :].rearrange("p b c -> p (b c)"),
                                  routersT[:, k, 0:NM], start=(k == 0), stop=(k == NC - 1))
                    last.then_inc(mid_done, 1)

            step(Tile(None, 0, 3, NT))
            pe.wait_ge(enc_up_ready, 1)
            pe.wait_ge(enc_low_ready, 1)
            pe.wait_ge(g_low_saved, 1)
            for m in range(NC):
                at = slice(m * P, (m + 1) * P)
                mm(bank_wb[m][:, :], enc_up[:, at], g_parts, start=False, stop=False)
                mm(bank_wb[m][:, :], enc_low[0:HP, at], g_parts[0:HP, :], start=False, stop=True).then_inc(wb_done, 1)
            step(Tile(None, 1, 3, NT))
            run_tiles(pe, 3, NT, 2, NT, step)

            pe.wait_ge(a1_in, 16)
            pe.wait_ge(wb_saved, NC)
            for k in range(NC):
                last = nc.tensor.transpose(bank_a1[:, k * P:(k + 1) * P], a1_nat[:, k * P:(k + 1) * P], ident[:, :])
            last.then_inc(a1t_done, 1)

            def split_product(dst, lhs, rhs, cols, ready=None):
                parts = [(lhs[0], rhs[0]), (lhs[0], rhs[1]), (lhs[1], rhs[0])]
                for k in range(NC):
                    if ready is not None:
                        pe.wait_ge(ready, k + 1)
                    for part, (a, b) in enumerate(parts):
                        last = mm(dst, a(k), b[:, k, cols], start=(k == 0 and part == 0), stop=(k == NC - 1 and part == 2))
                return last

            def product_m1(d):
                at = slice(d * P, (d + 1) * P)
                split_product(bank[d][:, :], [lambda k, w=w: w[:, k, at] for w in (w_h, w_l)], (wb_h, wb_l),
                              slice(0, D), w_split).then_inc(m1_done, 1)

            product_m1(0)
            step(Tile(None, NT + 1, 3, NT))
            for d in range(1, NC):
                product_m1(d)
            pe.wait_ge(b1_split, 1 + NC)
            pe.wait_ge(mid_saved, NT)
            split_product(bank[4][:, :], [lambda k, b=b: b[:, k, :] for b in (b1_h, b1_l)], (wb_h, wb_l),
                          slice(0, D)).then_inc(m2_done, 1)

            def step2(t):
                u = t + 1
                if u.real:
                    pe.wait_ge(x2_in[u.slot], u.round(16, 16))
                    if u.after(1):
                        pe.wait_ge(xtl_ready, u.count())
                    for k in range(NC):
                        last = nc.tensor.transpose(bank_x[:, k * P:(k + 1) * P], xs[:, u.slot, k * P:(k + 1) * P], ident[:, :])
                    last.then_inc(xt_done, 1)

                def turn_gm():
                    u = t + 1
                    if u.real:
                        pe.wait_ge(gm_ready, u.count(1, 1))
                        if u.after(3):
                            pe.wait_ge(ghtl_ready, u.count(1, -2))
                        elif u.after(1):
                            pe.wait_ge(gmtl_ready, u.count())
                        nc.tensor.transpose(bank_g[:, P:2 * P], gm[:, u.slot, :, :].rearrange("p a n -> p (a n)"),
                                            ident[:, :]).then_inc(gmt_done, 1)

                def finish(between=None):
                    u = t - 2
                    if u.real:
                        pe.wait_ge(ghtl_ready, u.count(1, 1))
                        b_0, b_1 = slots[u.slot]
                        for dst, cols in ((b_0[:, L1C:NX0], slice(0, OA)), (b_1[:, 0:NX1], slice(OA, D))):
                            for lhs, rhs in ((ght_h, m2h), (ght_h, m2l), (ght_l, m2h)):
                                last = mm(dst, lhs[u.slot][:, :], rhs[:, cols], start=False, stop=False, skip_group_check=True)
                            last.then_inc(out_done, 1)
                            if between is not None and cols.start == 0:
                                between()

                def turn_gh():
                    b = t - 1
                    if b.real:
                        pe.wait_ge(gh_ready, b.count(1, 1))
                        if (b + 2).real:
                            pe.wait_ge(gmtl_ready, b.count(1, 3))
                        nc.tensor.transpose(bank_g[:, 0:P], gh[:, b.slot, :], ident[:, :]).then_inc(ght_done, 1)

                def multiply(u, h, between=()):
                    if h == 0:
                        pe.wait_ge(xtl_ready, u.count(1, 1))
                        if u.after(3):
                            pe.wait_ge(out_saved, u.count(1, -2))
                    for k in range(NC + 1):
                        for at, other in between:
                            if at == k:
                                other()
                        if k == NC:
                            break
                        for part, (lhs, rhs) in enumerate(((xth, mxh), (xth, mxl), (xtl, mxh))):
                            mm(slots[u.slot][h][:, 0:(NX0, NX1)[h]], lhs[u.slot][:, k, :], rhs[:, k, half_x[h]],
                               start=(k == 0 and part == 0), stop=False)
                    if h == 0:
                        pe.wait_ge(gmtl_ready, u.count(1, 1))
                    if u.n is None and u.c == 0:
                        pe.wait_ge(bml_ready, h + 1)
                        if h == 1:
                            pe.wait_ge(m2l_ready, 1)
                    for rhs in (bmh, bml):
                        last = mm(slots[u.slot][h][:, 0:(NX0, NX1)[h]], gmt[u.slot][:, :], rhs[:, half_x[h]],
                                  start=False, stop=(rhs is bml))
                    last.then_inc((l1_done, x_done)[h], 1)

                if t.last:
                    turn_gh()
                    finish()
                    multiply(t, 1)
                elif t.real:
                    multiply(t, 0, [(1, turn_gm), (1, finish)])
                    if (t + 1).last:
                        multiply(t + 1, 0, [(2, turn_gh)])
                        multiply(t, 1)
                    else:
                        multiply(t, 1, [(NC, turn_gh)])
                elif t.past:
                    finish(turn_gh)
                    for _ in range(KEEP_UP):
                        mm(bank_x[:, 0:P], ident[:, :], ident[:, :], start=True, stop=True)
                else:
                    turn_gm()
                    finish()

            step2(Tile(None, -1, 3, NT))
            for k in range(2):
                pe.wait_ge(b0_split[k], 1 + NC)
            pe.wait_ge(a1l_ready, 1)
            pe.wait_ge(wr1_split, 2)
            for h in range(2):
                split_product(bank_bm[h][:, 0:(NX0, NX1)[h]], [lambda k, b=b: b[:, k, :, :].rearrange("p a n -> p (a n)") for b in (b0_h, b0_l)],
                              (mxh, mxl), half_x[h], mxl_ready).then_inc(bm_done, 1)
            run_tiles(pe, 3, NT, 0, NT + 1, step2)


_INS = ["x", "itok_B_0_7", "itok_B_2182_4065", "_lenS", "L0_cond_W_sess", "L0_cond_b_sess", "L0_cond_W2", "L0_cond_b2",
        "L0_ffn_A", "L0_ffn_B", "L0_ffn_Wr", "L1_cond_W", "L1_cond_Wr", "L1_cond_A", "L1_cond_B", "L1_ffn_W_base",
        "L1_ffn_b_base", "L1_ffn_enc0", "L1_ffn_enc1", "L1_ffn_coefs0", "L1_ffn_coefs1", "L1_ffn_mask0", "L1_ffn_mask1"]


def half_irfft(n):
    t = np.arange(n)
    rows = [np.full(n, 1.0 / np.sqrt(n))]
    for m in range(1, (n - 1) // 2 + 1):
        angle = 2.0 * np.pi * ((m * t) % n) / n
        rows += [np.sqrt(2.0 / n) * np.cos(angle), np.sqrt(2.0 / n) * np.sin(angle)]
    if n % 2 == 0:
        rows.append(np.where(t % 2 == 0, 1.0, -1.0) / np.sqrt(n))
    return (0.5 * np.stack(rows)).astype(np.float32)


def kernel(**inputs):
    import concourse.bacc as bacc
    from concourse.bass_utils import run_bass_kernel_spmd

    nc = bacc.Bacc("TRN2", target_bir_lowering=False, num_devices=1)
    arrays = {}
    for name in _INS:
        a = np.ascontiguousarray(inputs[name])
        arrays[f"in_{name}"] = a
    arrays["in_dft"] = half_irfft(inputs["L1_ffn_W_base"].shape[0])
    args = [nc.dram_tensor(n, a.shape, mybir.dt.from_np(a.dtype), kind="ExternalInput").ap() for n, a in arrays.items()]
    out = nc.dram_tensor("out_0", arrays["in_x"].shape, mybir.dt.float32, kind="ExternalOutput").ap()
    adaln_ffn(nc, *args, out)
    r = run_bass_kernel_spmd(nc, [arrays], core_ids=[0])
    return r.results[0]["out_0"]
```
